# Optimizing a Trainium2 kernel written in Bass

```python
import numpy as np
import jax
import jax.numpy as jnp

def _softmax(x, axis=-1):
    return jax.nn.softmax(x, axis=axis)

def _gelu(x):
    return jax.nn.gelu(x, approximate=True)

def _silu(x):
    return jax.nn.silu(x)

def _sigmoid(x):
    return jax.nn.sigmoid(x)

def _layernorm(x, axis=-1, eps=1e-05):
    m = jnp.mean(x, axis=axis, keepdims=True)
    v = jnp.var(x, axis=axis, keepdims=True)
    return (x - m) / jnp.sqrt(v + eps)

def _scatter_add(tgt, idx, src, axis=0):
    return tgt.at[idx].add(src)

def _segment_sum(src, seg, n):
    return jax.ops.segment_sum(src, seg, n)
kernel_name = 'mk_adj_resnorm_d4_adj_r2_9be00d'

def setup_inputs(seed: int=0):
    np.random.seed(seed)
    _w = jnp.asarray

    def _rec_inputs():
        import jax
        import jax.numpy as jnp
        _gk = jax.random.key(seed)
        x = -0.0002928 + 1 * jax.random.normal(jax.random.fold_in(_gk, 1), (32, 256, 256), jnp.float32)
        _a = jax.random.bernoulli(jax.random.fold_in(_gk, 2), 0.03125, (256, 256))
        _a = jnp.logical_or(_a, jnp.swapaxes(_a, -1, -2))
        _a = jnp.logical_or(_a, jnp.eye(256, dtype=bool))
        adj = _a.astype(jnp.int32)
        return (x, adj)
    x, adj = _rec_inputs()

    def _L0_gnn_setup():
        import jax, jax.numpy as jnp
        import numpy as np
        D_MODEL = 256
        NUM_HEADS = 8
        D_HEAD = D_MODEL // NUM_HEADS
        B, N = (4, 1024)
        key = jax.random.key(seed)
        ks = jax.random.split(key, 10)
        s = 1.0 / np.sqrt(D_MODEL)
        inp = {'h': jax.random.normal(ks[0], (B, N, D_MODEL), dtype=jnp.float32), 'adj': jax.random.randint(ks[1], (N, N), 0, 2, dtype=jnp.int32), 'Wq': jax.random.uniform(ks[2], (D_MODEL, D_MODEL), jnp.float32, -s, s), 'bq': jax.random.uniform(ks[3], (D_MODEL,), jnp.float32, -s, s), 'Wk': jax.random.uniform(ks[4], (D_MODEL, D_MODEL), jnp.float32, -s, s), 'bk': jax.random.uniform(ks[5], (D_MODEL,), jnp.float32, -s, s), 'Wv': jax.random.uniform(ks[6], (D_MODEL, D_MODEL), jnp.float32, -s, s), 'bv': jax.random.uniform(ks[7], (D_MODEL,), jnp.float32, -s, s), 'Wo': jax.random.uniform(ks[8], (D_MODEL, D_MODEL), jnp.float32, -s, s), 'bo': jax.random.uniform(ks[9], (D_MODEL,), jnp.float32, -s, s)}
        return inp
    _L0_gnn_all = _L0_gnn_setup()
    _L0_gnn_in = {k: v for k, v in _L0_gnn_all.items() if k in ('Wq', 'bq', 'Wk', 'bk', 'Wv', 'bv', 'Wo', 'bo')}
    del _L0_gnn_all

    def _L1_gnn_setup():
        import jax, jax.numpy as jnp
        import numpy as np
        B, K, DIN, DOUT = (32, 64, 256, 256)
        key = jax.random.key(seed)
        k1, k2, k3, k4 = jax.random.split(key, 4)
        x = jax.random.normal(k1, (B, K, DIN), dtype=jnp.float32)
        adj = jax.random.randint(k2, (K, K), 0, 2, dtype=jnp.int32)
        W = jax.random.normal(k3, (DOUT, 2 * DIN), dtype=jnp.float32) * 0.02
        b = jax.random.normal(k4, (DOUT,), dtype=jnp.float32) * 0.02
        return {'x': x, 'adj': adj, 'W': W, 'b': b}
    _L1_gnn_all = _L1_gnn_setup()
    _L1_gnn_in = {k: v for k, v in _L1_gnn_all.items() if k in ('W', 'b')}
    del _L1_gnn_all

    def _L2_gnn_setup():
        import jax, jax.numpy as jnp
        import numpy as np
        B, N, D = (8, 1024, 256)
        NEG_SLOPE = 0.2
        key = jax.random.key(seed)
        k1, k2, k3, k4, k5 = jax.random.split(key, 5)
        x = jax.random.normal(k1, (B, N, D), dtype=jnp.float32)
        adj = jax.random.randint(k2, (N, N), 0, 2, dtype=jnp.int32)
        adj = jnp.maximum(adj, jnp.eye(N, dtype=jnp.int32))
        W = jax.random.normal(k3, (D, D), dtype=jnp.float32) * (1.0 / np.sqrt(D))
        a_src = jax.random.normal(k4, (D,), dtype=jnp.float32) * (1.0 / np.sqrt(D))
        a_dst = jax.random.normal(k5, (D,), dtype=jnp.float32) * (1.0 / np.sqrt(D))
        return {'x': x, 'adj': adj, 'W': W, 'a_src': a_src, 'a_dst': a_dst}
    _L2_gnn_all = _L2_gnn_setup()
    _L2_gnn_in = {k: v for k, v in _L2_gnn_all.items() if k in ('W', 'a_src', 'a_dst')}
    del _L2_gnn_all

    def _L3_gnn_setup():
        import jax, jax.numpy as jnp
        import numpy as np
        LEAKY_ALPHA = 0.01
        NEG_INF = -1000000000.0
        LN_EPS = 1e-05

        def _gat_heads(x, adj, W, a):
            O = W.shape[-1]
            Wh = jnp.einsum('bnf,hfo->bhno', x, W)
            f1 = jnp.einsum('bhno,ho->bhn', Wh, a[:, :O])
            f2 = jnp.einsum('bhno,ho->bhn', Wh, a[:, O:])
            e = f1[:, :, :, None] + f2[:, :, None, :]
            e = jnp.where(e > 0, e, LEAKY_ALPHA * e)
            e = jnp.where(adj[None, None] > 0, e, NEG_INF)
            attn = jax.nn.softmax(e, axis=-1)
            return jnp.einsum('bhnm,bhmo->bhno', attn, Wh)
        key = jax.random.key(seed)
        ks = jax.random.split(key, 10)
        B, N, F_in, F_hid, H, F_out, D_ff = (8, 1024, 256, 256, 4, 256, 256)
        s = 0.05
        return {'enc_inputs': jax.random.normal(ks[0], (B, N, F_in), jnp.float32), 'adj': jax.random.randint(ks[1], (N, N), 0, 2, jnp.int32), 'W_heads': jax.random.normal(ks[2], (H, F_in, F_hid), jnp.float32) * s, 'a_heads': jax.random.normal(ks[3], (H, 2 * F_hid), jnp.float32) * s, 'W_out': jax.random.normal(ks[4], (H * F_hid, F_out), jnp.float32) * s, 'a_out': jax.random.normal(ks[5], (2 * F_out,), jnp.float32) * s, 'w1': jax.random.normal(ks[6], (F_out, D_ff), jnp.float32) * s, 'b1': jnp.zeros((D_ff,), jnp.float32), 'w2': jax.random.normal(ks[7], (D_ff, F_out), jnp.float32) * s, 'b2': jnp.zeros((F_out,), jnp.float32), 'ln_gamma': jnp.ones((F_out,), jnp.float32), 'ln_beta': jnp.zeros((F_out,), jnp.float32)}
    _L3_gnn_all = _L3_gnn_setup()
    _L3_gnn_in = {k: v for k, v in _L3_gnn_all.items() if k in ('W_heads', 'a_heads', 'W_out', 'a_out', 'w1', 'b1', 'w2', 'b2', 'ln_gamma', 'ln_beta')}
    del _L3_gnn_all
    return {'x': x, 'adj': adj, 'L0_gnn_Wq': _L0_gnn_in['Wq'], 'L0_gnn_bq': _L0_gnn_in['bq'], 'L0_gnn_Wk': _L0_gnn_in['Wk'], 'L0_gnn_bk': _L0_gnn_in['bk'], 'L0_gnn_Wv': _L0_gnn_in['Wv'], 'L0_gnn_bv': _L0_gnn_in['bv'], 'L0_gnn_Wo': _L0_gnn_in['Wo'], 'L0_gnn_bo': _L0_gnn_in['bo'], 'L1_gnn_W': _L1_gnn_in['W'], 'L1_gnn_b': _L1_gnn_in['b'], 'L2_gnn_W': _L2_gnn_in['W'], 'L2_gnn_a_src': _L2_gnn_in['a_src'], 'L2_gnn_a_dst': _L2_gnn_in['a_dst'], 'L3_gnn_W_heads': _L3_gnn_in['W_heads'], 'L3_gnn_a_heads': _L3_gnn_in['a_heads'], 'L3_gnn_W_out': _L3_gnn_in['W_out'], 'L3_gnn_a_out': _L3_gnn_in['a_out'], 'L3_gnn_w1': _L3_gnn_in['w1'], 'L3_gnn_b1': _L3_gnn_in['b1'], 'L3_gnn_w2': _L3_gnn_in['w2'], 'L3_gnn_b2': _L3_gnn_in['b2'], 'L3_gnn_ln_gamma': _L3_gnn_in['ln_gamma'], 'L3_gnn_ln_beta': _L3_gnn_in['ln_beta']}

def reference(x, adj, L0_gnn_Wq, L0_gnn_bq, L0_gnn_Wk, L0_gnn_bk, L0_gnn_Wv, L0_gnn_bv, L0_gnn_Wo, L0_gnn_bo, L1_gnn_W, L1_gnn_b, L2_gnn_W, L2_gnn_a_src, L2_gnn_a_dst, L3_gnn_W_heads, L3_gnn_a_heads, L3_gnn_W_out, L3_gnn_a_out, L3_gnn_w1, L3_gnn_b1, L3_gnn_w2, L3_gnn_b2, L3_gnn_ln_gamma, L3_gnn_ln_beta):
    import jax
    import jax.numpy as jnp

    def _L0_gnn_ref(h, adj, Wq, bq, Wk, bk, Wv, bv, Wo, bo):
        import jax, jax.numpy as jnp
        import numpy as np
        D_MODEL = 256
        NUM_HEADS = 8
        D_HEAD = D_MODEL // NUM_HEADS
        B, N = (4, 1024)
        b, n, _ = h.shape

        def split_heads(x):
            return x.reshape(b, n, NUM_HEADS, D_HEAD).transpose(0, 2, 1, 3)
        q = split_heads(h @ Wq.T + bq)
        k = split_heads(h @ Wk.T + bk)
        v = split_heads(h @ Wv.T + bv)
        scale = 1.0 / np.sqrt(D_HEAD)
        scores = jnp.einsum('bhqd,bhkd->bhqk', q, k) * scale
        mask = (adj == 0)[None, None, :, :]
        scores = jnp.where(mask, -jnp.inf, scores)
        attn = jax.nn.softmax(scores, axis=-1)
        out = jnp.einsum('bhqk,bhkd->bhqd', attn, v)
        out = out.transpose(0, 2, 1, 3).reshape(b, n, D_MODEL)
        return out @ Wo.T + bo

    def _L1_gnn_ref(x, adj, W, b):
        import jax, jax.numpy as jnp
        import numpy as np
        B, K, DIN, DOUT = (32, 64, 256, 256)
        Din = x.shape[-1]
        Wi, Wj = (W[:, :Din], W[:, Din:])
        mi = jnp.einsum('bkd,od->bko', x, Wi)
        mj = jnp.einsum('bkd,od->bko', x, Wj)
        a = adj.astype(x.dtype)
        deg = a.sum(axis=1)
        out = deg[None, :, None] * (mi + b) + jnp.einsum('ij,bjo->bio', a, mj)
        return out

    def _L2_gnn_ref(x, adj, W, a_src, a_dst):
        import jax, jax.numpy as jnp
        import numpy as np
        B, N, D = (8, 1024, 256)
        NEG_SLOPE = 0.2
        Wh = jnp.einsum('bnd,de->bne', x, W)
        e_src = jnp.einsum('bnd,d->bn', Wh, a_src)
        e_dst = jnp.einsum('bnd,d->bn', Wh, a_dst)
        logits = e_src[:, :, None] + e_dst[:, None, :]
        logits = jnp.where(logits >= 0, logits, NEG_SLOPE * logits)
        mask = (adj == 0)[None, :, :]
        logits = jnp.where(mask, -jnp.inf, logits)
        attn = jax.nn.softmax(logits, axis=-1)
        attn = jnp.nan_to_num(attn, nan=0.0)
        out = jnp.einsum('bnm,bmd->bnd', attn, Wh)
        return out

    def _L3_gnn_ref(enc_inputs, adj, W_heads, a_heads, W_out, a_out, w1, b1, w2, b2, ln_gamma, ln_beta):
        import jax, jax.numpy as jnp
        import numpy as np
        LEAKY_ALPHA = 0.01
        NEG_INF = -1000000000.0
        LN_EPS = 1e-05

        def _gat_heads(x, adj, W, a):
            O = W.shape[-1]
            Wh = jnp.einsum('bnf,hfo->bhno', x, W)
            f1 = jnp.einsum('bhno,ho->bhn', Wh, a[:, :O])
            f2 = jnp.einsum('bhno,ho->bhn', Wh, a[:, O:])
            e = f1[:, :, :, None] + f2[:, :, None, :]
            e = jnp.where(e > 0, e, LEAKY_ALPHA * e)
            e = jnp.where(adj[None, None] > 0, e, NEG_INF)
            attn = jax.nn.softmax(e, axis=-1)
            return jnp.einsum('bhnm,bhmo->bhno', attn, Wh)
        B, N, _ = enc_inputs.shape
        h = jax.nn.elu(_gat_heads(enc_inputs, adj, W_heads, a_heads))
        h = jnp.transpose(h, (0, 2, 1, 3)).reshape(B, N, -1)
        out = _gat_heads(h, adj, W_out[None], a_out[None])[:, 0]
        out = jax.nn.elu(out)
        ffn = jnp.maximum(out @ w1 + b1, 0.0) @ w2 + b2
        y = ffn + out
        mu = jnp.mean(y, axis=-1, keepdims=True)
        var = jnp.var(y, axis=-1, keepdims=True)
        return (y - mu) / jnp.sqrt(var + LN_EPS) * ln_gamma + ln_beta
    x = _layernorm(x + _L0_gnn_ref(x, adj, L0_gnn_Wq, L0_gnn_bq, L0_gnn_Wk, L0_gnn_bk, L0_gnn_Wv, L0_gnn_bv, L0_gnn_Wo, L0_gnn_bo), axis=-1)
    x = _layernorm(x + _L1_gnn_ref(x, adj, L1_gnn_W, L1_gnn_b), axis=-1)
    x = _layernorm(x + _L2_gnn_ref(x, adj, L2_gnn_W, L2_gnn_a_src, L2_gnn_a_dst), axis=-1)
    x = _layernorm(x + _L3_gnn_ref(x, adj, L3_gnn_W_heads, L3_gnn_a_heads, L3_gnn_W_out, L3_gnn_a_out, L3_gnn_w1, L3_gnn_b1, L3_gnn_w2, L3_gnn_b2, L3_gnn_ln_gamma, L3_gnn_ln_beta), axis=-1)
    return x

_drawn_inputs = setup_inputs


def setup_inputs(seed=0):
    import zlib

    import numpy as np

    out = dict(_drawn_inputs(seed))
    spreads = {'L3_gnn_b1': (0.0, 0.1),
     'L3_gnn_b2': (0.0, 0.1),
     'L3_gnn_ln_gamma': (1.0, 0.2),
     'L3_gnn_ln_beta': (0.0, 0.1)}
    factors = {'L0_gnn_bq': 8.0, 'L0_gnn_bk': 8.0}
    for name, (base, spread) in spreads.items():
        noise = np.random.default_rng([zlib.crc32(name.encode()), seed]).standard_normal(out[name].shape)
        drawn = base * np.exp(spread * noise) if base else spread * noise
        out[name] = jnp.asarray(drawn.astype(out[name].dtype))
    for name, factor in factors.items():
        out[name] = (out[name] * factor).astype(out[name].dtype)
    return out
```

```python
from contextlib import ExitStack

import concourse.bass as bass
from concourse import mybir

F32 = mybir.dt.float32
I32 = mybir.dt.int32
ALU = mybir.AluOpType
ACT = mybir.ActivationFunctionType
AX_X = mybir.AxisListType.X

P = 128
EPS = 1e-5
MASKED = -1e30
HUGE = 3e38


class Signal:

    def __init__(self, sem, per_graph=1, credit=0, step=1):
        self.sem, self.n, self.credit, self.step = sem, per_graph, credit, step

    def at(self, g, k=None):
        k = self.n - 1 if k is None else k
        return g * (self.n * self.step) + (self.credit + k + 1) * self.step


def interleave(*streams):
    keyed = [((i + 0.5) / len(s), j, x) for j, s in enumerate(streams) for i, x in enumerate(s)]
    return [x for _, _, x in sorted(keyed, key=lambda t: (t[0], t[1]))]


def attention_steps(load, heads, tail):
    out = list(load)
    for t in range(heads + 3):
        if t < heads:
            out.append(("scores", t))
        if 0 <= t - 1 < heads:
            out.append(("normalise", t - 1))
        if 0 <= t - 2 < heads:
            out.append(("turn", t - 2))
        if 0 <= t - 3 < heads:
            out.append(("mix", t - 3))
    return out + list(tail)


def build(nc, x, adj, Wq, bq, Wk, bk, Wv, bv, Wo, bo, W1i, W1j, b1m, W2, a2s, a2d,
          W3, a3, Wout, aout, Wf1, bf1, Wf2, bf2, gamma, beta, out):
    G, N, D = x.shape
    NC = N // P
    DC = D // P
    H0 = 8
    DH = D // H0
    HG = P // DH
    H3 = W3.shape[0]
    HC = H3 * DC
    SCALE = float(DH) ** -0.5
    SLOPE2, SLOPE3 = 0.2, 0.01

    A = [("a", *s) for s in attention_steps(
        [("x", 0), ("q", 0), ("k", 0), ("v", 0)], H0, [("out", 0)])]
    B = [("b", s, 0) for s in ("x", "near", "sum", "x2", "f", "scores", "turn", "mix", "out")]
    C = [("c", *s) for s in attention_steps([("x", 0), ("f", 0)], H3, [])]
    C = [s for c in C for s in ([c, ("c", "head", c[2])] if c[1] == "mix" else [c])]
    C += [("c", s, 0) for s in ("join", "scores5", "turn5", "mix5", "x5", "ffn1", "ffn2")]
    ORDER = interleave(A, B, C)
    assert ORDER.index(("a", "out", 0)) > ORDER.index(("b", "near", 0))
    assert ORDER.index(("b", "out", 0)) > ORDER.index(("c", "mix", H3 - 1))

    with ExitStack() as ctx:
        def sb(name, shape, dt=F32):
            return ctx.enter_context(nc.sbuf_tensor(name, shape, dt))

        def signal(name, per_graph=1, credit=0, step=1):
            return Signal(ctx.enter_context(nc.semaphore(name)), per_graph, credit, step)

        def bank(name):
            return ctx.enter_context(nc.psum_tensor(name, [P, 2, 256], F32))

        bk_at, bk_as, bk_ao = bank("bk_at"), bank("bk_as"), bank("bk_ao")
        bk_b0, bk_b1 = bank("bk_b0"), bank("bk_b1")
        bk_c0, bk_c1, bk_c2 = bank("bk_c0"), bank("bk_c1"), bank("bk_c2")

        ident, ones = sb("ident", [P, P]), sb("ones", [P, P])
        minus_half = sb("minus_half", [P, NC])
        adj_i = sb("adj_i", [P, NC, N], I32)
        adj_f = sb("adj_f", [P, NC, N])
        adjT = sb("adjT", [P, NC, N])
        neg = sb("neg", [P, NC, N])
        deg = sb("deg", [P, NC])
        wq, wk, wv, wo = (sb(n, [P, DC, D]) for n in ("wq", "wk", "wv", "wo"))
        bqc, bkc, bvc, bf1c = (sb(n, [P, DC]) for n in ("bqc", "bkc", "bvc", "bf1c"))
        bor, b1r, bf2r, gammar, betar = (sb(n, [P, D]) for n in ("bor", "b1r", "bf2r", "gammar", "betar"))
        bv_wide = sb("bv_wide", [P, DC, P])
        attn_bias = sb("attn_bias", [P, D])
        deg_bias = sb("deg_bias", [P, NC, D])
        w1i, w1j, w2, wf1, wf2 = (sb(n, [P, DC, D]) for n in ("w1i", "w1j", "w2", "wf1", "wf2"))
        w3 = sb("w3", [P, DC, H3, D])
        w5 = sb("w5", [P, HC, D + 2])
        a2r = sb("a2r", [P, 2, D])
        a3r = sb("a3r", [P, H3, 2, D])
        a5r = sb("a5r", [P, 2, D])
        u2 = sb("u2", [P, DC, 2])
        u3 = sb("u3", [P, DC, H3, 2])
        scratch = sb("scratch", [P, D])

        a_x, a_xT, a_q, a_k, a_v, a_res = (sb(n, [P, 2, 256]) for n in
                                           ("a_x", "a_xT", "a_q", "a_k", "a_v", "a_res"))
        a_s, a_p, a_pn, a_pT = (sb(n, [P, 2, 2, 256]) for n in ("a_s", "a_p", "a_pn", "a_pT"))
        a_max, a_sum, a_inv = (sb(n, [P, 2, NC]) for n in ("a_max", "a_sum", "a_inv"))
        a_oT = sb("a_oT", [P, 2, 256])
        a_y, x1 = sb("a_y", [P, NC, D]), sb("x1", [P, NC, D])
        b_xT, b_near, b_res, b_t, b_y, x2, b_x2T = (sb(n, [P, 2, 256]) for n in
                                                    ("b_xT", "b_near", "b_res", "b_t", "b_y", "x2", "b_x2T"))
        b_f, b_diag = sb("b_f", [P, NC, 2]), sb("b_diag", [P, NC, P])
        b_s, b_p, b_pT, b_mix, b_y2, x3 = (sb(n, [P, 2, 256]) for n in
                                                ("b_s", "b_p", "b_pT", "b_mix", "b_y2", "x3"))
        b_nf = sb("b_nf", [P, NC, N])
        b_min, b_nm, b_sum, b_inv = (sb(n, [P, NC]) for n in ("b_min", "b_nm", "b_sum", "b_inv"))
        c_xT, c_res = sb("c_xT", [P, 2, 256]), sb("c_res", [P, NC, D])
        c_f, c_diag = sb("c_f", [P, NC, H3, 2]), sb("c_diag", [P, NC, H3, P])
        c_s, c_p, c_pn, c_pT, c_mix, c_e = (sb(n, [P, 2, 2, 256]) for n in
                                            ("c_s", "c_p", "c_pn", "c_pT", "c_mix", "c_e"))
        c_nf = sb("c_nf", [P, 2, NC, N])
        c_min, c_nm, c_sum, c_inv = (sb(n, [P, 2, NC]) for n in ("c_min", "c_nm", "c_sum", "c_inv"))
        c_hT = sb("c_hT", [P, HC, 256])
        c_h2 = sb("c_h2", [P, NC, D + 2])
        c_diag5 = sb("c_diag5", [P, NC, P])
        c_s5, c_p5, c_pT5, c_e5, c_o5, c_o5T, c_res5, c_hid, c_y, c_n, c_ng, c_z, c_out = (
            sb(n, [P, 2, 256]) for n in ("c_s5", "c_p5", "c_pT5", "c_e5", "c_o5", "c_o5T", "c_res5",
                                         "c_hid", "c_y", "c_n", "c_ng", "c_z", "c_out"))
        c_nf5 = sb("c_nf5", [P, NC, N])
        c_min5, c_nm5, c_sum5, c_inv5 = (sb(n, [P, NC]) for n in ("c_min5", "c_nm5", "c_sum5", "c_inv5"))

        class Norm:

            def __init__(self, name):
                self.stats = sb(f"{name}_stats", [P, NC, 6])
                self.mv = sb(f"{name}_mv", [P, NC, 2])
                self.ve = sb(f"{name}_ve", [P, NC])
                self.rstd = sb(f"{name}_rstd", [P, NC])
                self.in_ready = signal(f"{name}_in_ready", 1, 1)
                self.stats_ready = signal(f"{name}_stats_ready")
                self.mv_ready = signal(f"{name}_mv_ready")
                self.ve_ready = signal(f"{name}_ve_ready")
                self.rstd_ready = signal(f"{name}_rstd_ready")
                self.done = signal(f"{name}_done")

        n0, n1, n2, n3, n4 = (Norm(f"norm{i}") for i in range(5))

        a_loaded, b_loaded, c_loaded = signal("a_loaded"), signal("b_loaded"), signal("c_loaded")
        ident_set, consts_set = signal("ident_set"), signal("consts_set")
        adjf_set, neg_set, bvw_set = signal("adjf_set"), signal("neg_set"), signal("bvw_set")
        adjT_in, adjT_set, ab_in, ab_set = signal("adjT_in"), signal("adjT_set"), signal("ab_in"), signal("ab_set")
        u2_set, u3_set, u5_set, db_set = signal("u2_set"), signal("u3_set"), signal("u5_set"), signal("db_set")
        scr = signal("scratch_written")
        x_loaded = signal("x_loaded", step=16)
        xT_in, xT_set, q_in, q_set, k_in, k_set, v_in, v_set = (
            signal(n) for n in ("xT_in", "xT_set", "q_in", "q_set", "k_in", "k_set", "v_in", "v_set"))
        a_res_set = signal("a_res_set")
        s_in, s_set, p_set, inv_set = (signal(n, H0) for n in ("s_in", "s_set", "p_set", "inv_set"))
        pn_set, pT_in, pT_set = (signal(n, H0, 2) for n in ("pn_set", "pT_in", "pT_set"))
        o_in = signal("o_in", H0)
        oT_set, ao_in = signal("oT_set", 1, 1), signal("ao_in")
        bxT_in, bxT_set, near_in, b_res_set = signal("bxT_in"), signal("bxT_set"), signal("near_in", 1, 1), signal("b_res_set", 1, 1)
        near_set, yi_in, yj_in, yi_read = (signal(n) for n in ("near_set", "yi_in", "yj_in", "yi_read"))
        x2T_in, x2T_set, bf_in, bf_set, bd_set = (signal(n) for n in ("x2T_in", "x2T_set", "bf_in", "bf_set", "bd_set"))
        bs_in, bnf_set, bs_set, bnm_set, bp_set, binv_set = (
            signal(n) for n in ("bs_in", "bnf_set", "bs_set", "bnm_set", "bp_set", "binv_set"))
        bpT_in, bpT_set, bm_in, bm_set, bo_in = (
            signal("bpT_in"), signal("bpT_set"), signal("bm_in"), signal("bm_set", 1, 1), signal("bo_in"))
        cxT_in, cxT_set, cf_in, cf_set, cd_set, c_res_set = (
            signal("cxT_in"), signal("cxT_set"), signal("cf_in"), signal("cf_set"), signal("cd_set"), signal("c_res_set", 1, 1))
        cs_in, cnf_set, cnm_set, cp_set, cinv_set = (
            signal(n, H3) for n in ("cs_in", "cnf_set", "cnm_set", "cp_set", "cinv_set"))
        cs_set = signal("cs_set", H3, 2)
        cpn_set, cpT_in = signal("cpn_set", H3, 2), signal("cpT_in", H3, 2)
        cpT_set, cm_in, cm_set, ch_in, ce_set, cg_set, ch_set = (
            signal(n, H3, 1 if n == "cm_in" else 0) for n in ("cpT_set", "cm_in", "cm_set", "ch_in", "ce_set", "cg_set", "ch_set"))
        h2_in, h2a_set, h2b_set, d5_set = signal("h2_in"), signal("h2a_set"), signal("h2b_set"), signal("d5_set")
        s5_in, nf5_set, s5_set, nm5_set, p5_set, inv5_set = (
            signal(n) for n in ("s5_in", "nf5_set", "s5_set", "nm5_set", "p5_set", "inv5_set"))
        pT5_in, pT5_set, m5_in, e5_set, g5_set, o5_set = (
            signal(n) for n in ("pT5_in", "pT5_set", "m5_in", "e5_set", "g5_set", "o5_set"))
        o5T_in, o5T_set, res5_set, hid_in, hid_set, y_in = (
            signal("o5T_in"), signal("o5T_set", 1, 1), signal("res5_set"), signal("hid_in"), signal("hid_set", 1, 1),
            signal("y_in"))
        ng_set = signal("ng_set")
        stored = signal("stored", 1, 1, step=16)

        block = ctx.enter_context(nc.Block())

        def run(eng, steps):
            def iteration(a, b, c):
                graph = {"a": a, "b": b, "c": c}
                for stream, what, k in ORDER:
                    if graph[stream] is not None and (stream, what) in steps:
                        steps[stream, what](graph[stream], k)

            iteration(0, None, None)
            iteration(1, 0, None)
            with eng.Fori(2, G) as i:
                iteration(i, i - 1, i - 2)
            iteration(None, G - 1, G - 2)
            iteration(None, None, G - 1)

        rows = lambda w: w.rearrange("(c p) o -> p c o", p=P)
        wide = lambda v: v.partition_broadcast(P)

        def graph_rows(t, g):
            return t.rearrange("g (c p) f -> g p c f", p=P)[g]

        def grant(eng, *signals):
            for sig in signals:
                eng.sem_inc(sig.sem, sig.credit * sig.step)

        passed = {}

        def wait_apart(eng, *waits):
            for sig, value in waits:
                eng.wait_ge(sig.sem, value)
            eng.sem_inc(passed[eng], 1)

        @block.sync
        def _(sp):
            grant(sp, stored)
            loads_a = [(adj_i[:], rows(adj)), (wq[:], rows(Wq)), (bqc[:], bq), (wk[:], rows(Wk)),
                       (bkc[:], bk), (wv[:], rows(Wv)), (wo[:], rows(Wo)), (bvc[:], bv), (bor[:], wide(bo))]
            loads_b = [(w1i[:], rows(W1i)), (w1j[:], rows(W1j)), (b1r[:], wide(b1m)), (w2[:], rows(W2)),
                       (a2r[:, 0, :], wide(a2s)), (a2r[:, 1, :], wide(a2d))]
            loads_c = [(w3[:, :, h, :], rows(W3[h])) for h in range(H3)]
            loads_c += [(a3r[:], wide(a3.rearrange("h (t o) -> h t o", t=2))), (w5[:, :, 0:D], rows(Wout)),
                        (a5r[:], wide(aout.rearrange("(t o) -> t o", t=2))), (wf1[:], rows(Wf1)), (bf1c[:], bf1),
                        (wf2[:], rows(Wf2)), (bf2r[:], wide(bf2)), (gammar[:], wide(gamma)), (betar[:], wide(beta))]
            sp.dma_start(a_x[:], graph_rows(x, 0)).then_inc(x_loaded.sem, 16)
            for sig, loads in ((a_loaded, loads_a), (b_loaded, loads_b), (c_loaded, loads_c)):
                for dst, src in loads:
                    sp.dma_start(dst, src).then_inc(sig.sem, 16)

            def load_next(g, _):
                sp.wait_ge(xT_in.sem, xT_in.at(g))
                sp.wait_ge(a_res_set.sem, a_res_set.at(g))
                sp.dma_start(a_x[:], graph_rows(x, g + 1)).then_inc(x_loaded.sem, 16)

            def store(g, _):
                sp.wait_ge(n4.done.sem, n4.done.at(g))
                sp.dma_start(graph_rows(out, g), c_out[:]).then_inc(stored.sem, 16)

            load_next(0, 0)
            load_next(1, 0)
            with sp.Fori(2, G - 1) as i:
                load_next(i, 0)
                store(i - 2, 0)
            for g in range(G - 3, G):
                store(g, 0)
            sp.wait_ge(stored.sem, stored.at(G - 1))

        LOADED = {"a": 9 * 16, "b": 6 * 16, "c": (H3 + 9) * 16}

        @block.tensor
        def _(pe):
            def turn(dst, src):
                for r in range(2):
                    for c in range(2):
                        last = pe.transpose(dst[:, c, r * P:(r + 1) * P], src[:, r, c * P:(c + 1) * P], ident[:])
                return last

            def product(dst, lhsT, rhs, chunks=2):
                for m in range(2):
                    for k in range(chunks):
                        last = pe.matmul(dst[:, m, :], lhsT[:, k, m * P:(m + 1) * P], rhs[:, k, :],
                                         start=(k == 0), stop=(k == chunks - 1))
                return last

            grant(pe, near_in, cm_in, pT_in, cpT_in)
            pe.wait_ge(ident_set.sem, 1)
            pe.wait_ge(adjf_set.sem, 1)
            turn(bk_at, adj_f).then_inc(adjT_in.sem, 1)
            pe.wait_ge(bvw_set.sem, 1)
            for k in range(DC):
                last = pe.matmul(bk_as[:, 0, :], bv_wide[:, k, :], wo[:, k, :], start=(k == 0), stop=(k == DC - 1))
            last.then_inc(ab_in.sem, 1)
            pe.wait_ge(a_loaded.sem, LOADED["a"])
            pe.wait_ge(adjT_set.sem, 1)
            pe.wait_ge(ab_set.sem, 1)
            pe.wait_ge(consts_set.sem, 2)

            def ax(g, _):
                pe.wait_ge(x_loaded.sem, x_loaded.at(g))
                pe.wait_ge(pT_set.sem, pT_set.at(g, -1))
                turn(bk_at, a_x).then_inc(xT_in.sem, 1)

            def aq(g, _):
                pe.wait_ge(xT_set.sem, xT_set.at(g))
                pe.wait_ge(n0.in_ready.sem, n0.in_ready.at(g, -1))
                product(bk_as, wq, a_xT).then_inc(q_in.sem, 1)

            def ak(g, _):
                pe.wait_ge(oT_set.sem, oT_set.at(g, -1))
                product(bk_ao, wk, a_xT).then_inc(k_in.sem, 1)

            def av(g, _):
                product(bk_at, a_xT, wv).then_inc(v_in.sem, 1)

            def a_scores(g, h):
                if h == 0:
                    pe.wait_ge(q_set.sem, q_set.at(g))
                    pe.wait_ge(k_set.sem, k_set.at(g))
                else:
                    pe.wait_ge(s_set.sem, s_set.at(g, h - 1))
                r, c = (h % HG) * DH, h // HG
                for m in range(NC):
                    last = pe.matmul(bk_as[:, m, :], a_q[r:r + DH, c, m * P:(m + 1) * P], a_k[r:r + DH, c, :],
                                     start=True, stop=True)
                last.then_inc(s_in.sem, 1)

            def a_turn(g, h):
                if h == 0:
                    pe.wait_ge(v_set.sem, v_set.at(g))
                else:
                    pe.wait_ge(pT_set.sem, pT_set.at(g, h - 1))
                pe.wait_ge(pn_set.sem, pn_set.at(g, h))
                turn(bk_at, a_pn[:, h % 2]).then_inc(pT_in.sem, 1)

            def a_mix(g, h):
                pe.wait_ge(pT_set.sem, pT_set.at(g, h))
                r, c = (h % HG) * DH, h // HG
                for k in range(NC):
                    last = pe.matmul(bk_ao[r:r + DH, c, :], a_v[:, k, h * DH:(h + 1) * DH], a_pT[:, h % 2, k, :],
                                     start=(k == 0), stop=(k == NC - 1))
                last.then_inc(o_in.sem, 1)

            def a_out(g, _):
                pe.wait_ge(oT_set.sem, oT_set.at(g))
                pe.wait_ge(s_set.sem, s_set.at(g, H0 - 1))
                product(bk_as, a_oT, wo).then_inc(ao_in.sem, 1)

            def bx(g, _):
                pe.wait_ge(n0.done.sem, n0.done.at(g))
                pe.wait_ge(bm_set.sem, bm_set.at(g, -1))
                turn(bk_b0, x1).then_inc(bxT_in.sem, 1)

            def b_near_(g, _):
                pe.wait_ge(n2.in_ready.sem, n2.in_ready.at(g, -1))
                product(bk_b1, x1, adjT).then_inc(near_in.sem, 1)

            def b_sum_(g, _):
                pe.wait_ge(bxT_set.sem, bxT_set.at(g))
                product(bk_b0, b_xT, w1i).then_inc(yi_in.sem, 1)
                pe.wait_ge(near_set.sem, near_set.at(g))
                product(bk_b1, b_near, w1j).then_inc(yj_in.sem, 1)

            def bx2(g, _):
                pe.wait_ge(n1.done.sem, n1.done.at(g))
                turn(bk_b0, x2).then_inc(x2T_in.sem, 1)

            def bf(g, _):
                pe.wait_ge(x2T_set.sem, x2T_set.at(g))
                for m in range(NC):
                    for k in range(DC):
                        last = pe.matmul(bk_b1[:, 0, 2 * m:2 * m + 2], b_x2T[:, k, m * P:(m + 1) * P], u2[:, k, :],
                                         start=(k == 0), stop=(k == DC - 1))
                last.then_inc(bf_in.sem, 1)

            def spread(dst, diag):
                for k in range(NC):
                    last = pe.matmul(dst[:, k * P:(k + 1) * P], ones[:], diag[:, k, :], start=True, stop=True)
                return last

            def b_scores(g, _):
                pe.wait_ge(bd_set.sem, bd_set.at(g))
                spread(bk_b0[:, 0, :], b_diag).then_inc(bs_in.sem, 1)

            def b_turn(g, _):
                pe.wait_ge(bp_set.sem, bp_set.at(g))
                turn(bk_b1, b_p).then_inc(bpT_in.sem, 1)

            def b_mix_(g, _):
                pe.wait_ge(bpT_set.sem, bpT_set.at(g))
                product(bk_b0, x2, b_pT).then_inc(bm_in.sem, 1)

            def b_out(g, _):
                pe.wait_ge(bm_set.sem, bm_set.at(g))
                product(bk_b1, b_mix, w2).then_inc(bo_in.sem, 1)

            def cx(g, _):
                pe.wait_ge(n2.done.sem, n2.done.at(g))
                pe.wait_ge(hid_set.sem, hid_set.at(g, -1))
                turn(bk_c0, x3).then_inc(cxT_in.sem, 1)

            def cf(g, _):
                pe.wait_ge(cxT_set.sem, cxT_set.at(g))
                pe.wait_ge(n3.in_ready.sem, n3.in_ready.at(g, -1))
                w = 2 * H3
                for m in range(NC):
                    for k in range(DC):
                        last = pe.matmul(bk_c1[:, 0, w * m:w * m + w], c_xT[:, k, m * P:(m + 1) * P],
                                         u3[:, k, :, :].rearrange("p h t -> p (h t)"),
                                         start=(k == 0), stop=(k == DC - 1))
                last.then_inc(cf_in.sem, 1)

            def c_scores(g, h):
                if h == 0:
                    pe.wait_ge(cd_set.sem, cd_set.at(g))
                else:
                    pe.wait_ge(cs_set.sem, cs_set.at(g, h - 1))
                spread(bk_c0[:, 0, :], c_diag[:, :, h, :]).then_inc(cs_in.sem, 1)

            def c_turn(g, h):
                if h > 0:
                    pe.wait_ge(cpT_set.sem, cpT_set.at(g, h - 1))
                pe.wait_ge(cpn_set.sem, cpn_set.at(g, h))
                turn(bk_c1, c_pn[:, h % 2]).then_inc(cpT_in.sem, 1)

            def c_mix_(g, h):
                if h == 0:
                    pe.wait_ge(o5T_set.sem, o5T_set.at(g, -1))
                else:
                    pe.wait_ge(ch_set.sem, ch_set.at(g, h - 1))
                pe.wait_ge(cpT_set.sem, cpT_set.at(g, h))
                product(bk_c2, x3, c_pT[:, h % 2]).then_inc(cm_in.sem, 1)

            def c_head(g, h):
                pe.wait_ge(cm_set.sem, cm_set.at(g, h))
                product(bk_c2, w3[:, :, h, :], c_mix[:, h % 2]).then_inc(ch_in.sem, 1)

            def c_join(g, _):
                pe.wait_ge(ch_set.sem, ch_set.at(g))
                for m, dst in enumerate((bk_c0, bk_c1)):
                    flat = dst[:, :, :].rearrange("p a b -> p (a b)")[:, 0:D + 2]
                    for k in range(HC):
                        last = pe.matmul(flat, c_hT[:, k, m * P:(m + 1) * P], w5[:, k, :],
                                         start=(k == 0), stop=(k == HC - 1))
                last.then_inc(h2_in.sem, 1)

            def c_scores5(g, _):
                pe.wait_ge(d5_set.sem, d5_set.at(g))
                spread(bk_c0[:, 0, :], c_diag5).then_inc(s5_in.sem, 1)

            def c_turn5(g, _):
                pe.wait_ge(p5_set.sem, p5_set.at(g))
                pe.wait_ge(h2b_set.sem, h2b_set.at(g))
                turn(bk_c1, c_p5).then_inc(pT5_in.sem, 1)

            def c_mix5(g, _):
                pe.wait_ge(pT5_set.sem, pT5_set.at(g))
                product(bk_c2, c_pT5, c_h2[:, :, 0:D]).then_inc(m5_in.sem, 1)

            def c_x5(g, _):
                pe.wait_ge(o5_set.sem, o5_set.at(g))
                turn(bk_c2, c_o5).then_inc(o5T_in.sem, 1)

            def c_ffn1(g, _):
                pe.wait_ge(o5T_set.sem, o5T_set.at(g))
                product(bk_c0, wf1, c_o5T).then_inc(hid_in.sem, 1)

            def c_ffn2(g, _):
                pe.wait_ge(hid_set.sem, hid_set.at(g))
                product(bk_c1, c_hid, wf2).then_inc(y_in.sem, 1)

            def once(fn, *waits):
                def step(g, k):
                    if isinstance(g, int) and g == 0 and k == 0:
                        for sig, value in waits:
                            pe.wait_ge(sig.sem, value)
                    fn(g, k)
                return step

            run(pe, {
                ("a", "x"): ax, ("a", "q"): aq, ("a", "k"): ak, ("a", "v"): av, ("a", "scores"): a_scores,
                ("a", "turn"): a_turn, ("a", "mix"): a_mix, ("a", "out"): a_out,
                ("b", "x"): once(bx, (b_loaded, LOADED["b"]), (u2_set, 1)), ("b", "near"): b_near_, ("b", "sum"): b_sum_,
                ("b", "x2"): bx2, ("b", "f"): bf, ("b", "scores"): b_scores, ("b", "turn"): b_turn, ("b", "mix"): b_mix_,
                ("b", "out"): b_out,
                ("c", "x"): once(cx, (c_loaded, LOADED["c"]), (u3_set, 1), (u5_set, 1)), ("c", "f"): cf,
                ("c", "scores"): c_scores, ("c", "turn"): c_turn, ("c", "mix"): c_mix_, ("c", "head"): c_head,
                ("c", "join"): c_join, ("c", "scores5"): c_scores5, ("c", "turn5"): c_turn5, ("c", "mix5"): c_mix5,
                ("c", "x5"): c_x5, ("c", "ffn1"): c_ffn1, ("c", "ffn2"): c_ffn2,
            })

        @block.scalar
        def _(act):
            grant(act, pT_set, oT_set, bm_set, hid_set, o5T_set)
            act.wait_ge(adjT_in.sem, 1)
            act.activation(adjT[:], bk_at[:], ACT.Copy).then_inc(adjT_set.sem, 1)
            act.wait_ge(a_loaded.sem, LOADED["a"])

            def copy(dst, src, filled, value, done):
                act.wait_ge(filled.sem, value)
                act.activation(dst, src, ACT.Copy).then_inc(done.sem, 1)

            def ax(g, _):
                copy(a_xT[:], bk_at[:], xT_in, xT_in.at(g), xT_set)

            def ak(g, _):
                act.wait_ge(k_in.sem, k_in.at(g))
                for c in range(DC):
                    last = act.activation(a_k[:, c, :], bk_ao[:, c, :], ACT.Identity, bias=bkc[:, c:c + 1])
                last.then_inc(k_set.sem, 1)

            def av(g, _):
                copy(a_v[:], bk_at[:], v_in, v_in.at(g), v_set)

            def a_scores(g, h):
                act.wait_ge(s_set.sem, s_set.at(g, h))
                act.wait_ge(pn_set.sem, pn_set.at(g, h - 2))
                for m in range(NC):
                    last = act.activation(a_p[:, h % 2, m, :], a_s[:, h % 2, m, :], ACT.Exp,
                                          bias=a_max[:, h % 2, m:m + 1], scale=-1.0, accum_out=a_sum[:, h % 2, m:m + 1])
                last.then_inc(p_set.sem, 1)

            def a_turn(g, h):
                copy(a_pT[:, h % 2], bk_at[:], pT_in, pT_in.at(g, h), pT_set)

            def a_out(g, _):
                copy(a_oT[:], bk_ao[:], o_in, o_in.at(g), oT_set)

            def gat_probs(s, p, nm, total, done):
                for m in range(NC):
                    last = act.activation(p[:, m, :], s[:, m, :], ACT.Exp, bias=nm[:, m:m + 1], scale=-1.0,
                                          accum_out=total[:, m:m + 1])
                last.then_inc(done.sem, 1)

            def bx(g, _):
                copy(b_xT[:], bk_b0[:], bxT_in, bxT_in.at(g), bxT_set)

            def bx2(g, _):
                copy(b_x2T[:], bk_b0[:], x2T_in, x2T_in.at(g), x2T_set)

            def b_scores(g, _):
                act.wait_ge(bnm_set.sem, bnm_set.at(g))
                gat_probs(b_s, b_p, b_nm, b_sum, bp_set)

            def b_turn(g, _):
                copy(b_pT[:], bk_b1[:], bpT_in, bpT_in.at(g), bpT_set)

            def b_mix_(g, _):
                copy(b_mix[:], bk_b0[:], bm_in, bm_in.at(g), bm_set)

            def cx(g, _):
                copy(c_xT[:], bk_c0[:], cxT_in, cxT_in.at(g), cxT_set)

            def c_scores(g, h):
                act.wait_ge(cnm_set.sem, cnm_set.at(g, h))
                act.wait_ge(cpn_set.sem, cpn_set.at(g, h - 2))
                i = h % 2
                gat_probs(c_s[:, i], c_p[:, i], c_nm[:, i], c_sum[:, i], cp_set)

            def c_mix_(g, h):
                copy(c_mix[:, h % 2], bk_c2[:], cm_in, cm_in.at(g, h), cm_set)

            def c_head(g, h):
                act.wait_ge(ch_in.sem, ch_in.at(g, h))
                act.activation(c_e[:, h % 2], bk_c2[:], ACT.Exp).then_inc(ce_set.sem, 1)

            def c_join(g, _):
                act.wait_ge(h2_in.sem, h2_in.at(g))
                act.activation(c_h2[:, 1, :], bk_c1[:, :, :].rearrange("p a b -> p (a b)")[:, 0:D + 2],
                               ACT.Copy).then_inc(h2b_set.sem, 1)

            def c_scores5(g, _):
                act.wait_ge(nm5_set.sem, nm5_set.at(g))
                gat_probs(c_s5, c_p5, c_nm5, c_sum5, p5_set)

            def c_turn5(g, _):
                copy(c_pT5[:], bk_c1[:], pT5_in, pT5_in.at(g), pT5_set)

            def c_mix5(g, _):
                act.wait_ge(m5_in.sem, m5_in.at(g))
                act.wait_ge(inv5_set.sem, inv5_set.at(g))
                for m in range(NC):
                    last = act.activation(c_e5[:, m, :], bk_c2[:, m, :], ACT.Exp, scale=c_inv5[:, m:m + 1])
                last.then_inc(e5_set.sem, 1)

            def c_x5(g, _):
                copy(c_o5T[:], bk_c2[:], o5T_in, o5T_in.at(g), o5T_set)

            def c_ffn1(g, _):
                act.wait_ge(hid_in.sem, hid_in.at(g))
                for c in range(DC):
                    last = act.activation(c_hid[:, c, :], bk_c0[:, c, :], ACT.Relu, bias=bf1c[:, c:c + 1])
                last.then_inc(hid_set.sem, 1)

            def once(fn, sig, value):
                def step(g, k):
                    if isinstance(g, int) and g == 0:
                        act.wait_ge(sig.sem, value)
                    fn(g, k)
                return step

            run(act, {
                ("a", "x"): ax, ("a", "k"): ak, ("a", "v"): av, ("a", "scores"): a_scores, ("a", "turn"): a_turn,
                ("a", "out"): a_out,
                ("b", "x"): bx, ("b", "x2"): bx2, ("b", "scores"): b_scores, ("b", "turn"): b_turn, ("b", "mix"): b_mix_,
                ("c", "x"): once(cx, c_loaded, LOADED["c"]), ("c", "scores"): c_scores, ("c", "mix"): c_mix_,
                ("c", "head"): c_head, ("c", "join"): c_join,
                ("c", "scores5"): c_scores5, ("c", "turn5"): c_turn5, ("c", "mix5"): c_mix5, ("c", "x5"): c_x5,
                ("c", "ffn1"): c_ffn1,
            })

        @block.vector
        def _(dve):
            passed[dve] = ctx.enter_context(nc.semaphore("vector_waits_passed"))
            grant(dve, n0.in_ready, n1.in_ready, n2.in_ready, n3.in_ready, n4.in_ready, cs_set)
            dve.wait_ge(a_loaded.sem, LOADED["a"])
            dve.tensor_copy(adj_f[:], adj_i[:]).then_inc(adjf_set.sem, 1)
            dve.wait_ge(adjf_set.sem, 1)
            dve.tensor_scalar(neg[:], adj_f[:], 0.0, MASKED, ALU.is_equal, ALU.mult).then_inc(neg_set.sem, 1)
            dve.tensor_reduce(deg[:], adj_f[:], AX_X, ALU.add).then_inc(neg_set.sem, 1)
            dve.wait_ge(consts_set.sem, 2)
            for k in range(DC):
                last = dve.tensor_scalar(bv_wide[:, k, :], ones[:], bvc[:, k:k + 1], None, ALU.mult)
            last.then_inc(bvw_set.sem, 1)
            dve.wait_ge(ab_in.sem, 1)
            dve.tensor_tensor(attn_bias[:], bk_as[:, 0, :], bor[:], ALU.add).then_inc(ab_set.sem, 1)
            dve.wait_ge(neg_set.sem, 2)
            dve.wait_ge(ident_set.sem, 1)

            written = [0]

            def fold(dst, w, a):
                if written[0]:
                    dve.wait_ge(scr.sem, written[0])
                written[0] += 1
                return dve.tensor_tensor_reduce(scratch[:], w, a, 1.0, 0.0, ALU.mult, ALU.add, dst)

            def fold_b():
                dve.wait_ge(b_loaded.sem, LOADED["b"])
                for k in range(DC):
                    for t in range(2):
                        fold(u2[:, k, t:t + 1], w2[:, k, :], a2r[:, t, :]).then_inc(scr.sem, 1)
                for m in range(NC):
                    last = dve.tensor_scalar(deg_bias[:, m, :], b1r[:], deg[:, m:m + 1], None, ALU.mult)
                last.then_inc(db_set.sem, 1)
                dve.wait_ge(scr.sem, written[0])
                dve.sem_inc(u2_set.sem, 1)

            def fold_c():
                dve.wait_ge(c_loaded.sem, LOADED["c"])
                for k in range(DC):
                    for h in range(H3):
                        for t in range(2):
                            fold(u3[:, k, h, t:t + 1], w3[:, k, h, :], a3r[:, h, t, :]).then_inc(scr.sem, 1)
                for k in range(HC):
                    for t in range(2):
                        fold(w5[:, k, D + t:D + t + 1], w5[:, k, 0:D], a5r[:, t, :]).then_inc(scr.sem, 1)
                dve.wait_ge(scr.sem, written[0])
                dve.sem_inc(u3_set.sem, 1)
                dve.sem_inc(u5_set.sem, 1)

            def norm(n, g, src, dst, *free):
                dve.wait_ge(n.in_ready.sem, n.in_ready.at(g))
                for m in range(NC):
                    last = dve.bn_stats(n.stats[:, m, :], src[:, m, :])
                last.then_inc(n.stats_ready.sem, 1)
                wait_apart(dve, (n.stats_ready, n.stats_ready.at(g)))
                for m in range(NC):
                    last = dve.bn_aggr(n.mv[:, m, :], n.stats[:, m, :])
                last.then_inc(n.mv_ready.sem, 1)
                dve.wait_ge(n.mv_ready.sem, n.mv_ready.at(g))
                dve.tensor_scalar(n.ve[:], n.mv[:, :, 1], EPS, None, ALU.add).then_inc(n.ve_ready.sem, 1)
                dve.wait_ge(n.rstd_ready.sem, n.rstd_ready.at(g))
                for sig, value in free:
                    dve.wait_ge(sig.sem, value)
                for m in range(NC):
                    last = dve.tensor_scalar(dst[:, m, :], src[:, m, :], n.mv[:, m, 0:1], n.rstd[:, m:m + 1],
                                             ALU.subtract, ALU.mult)
                last.then_inc(n.done.sem, 1)

            def aq(g, _):
                dve.wait_ge(q_in.sem, q_in.at(g))
                dve.tensor_tensor(a_q[:], bk_as[:], bqc[:].unsqueeze(2).to_broadcast([P, DC, N]),
                                  ALU.add).then_inc(q_set.sem, 1)

            def a_scores(g, h):
                wait_apart(dve, (s_in, s_in.at(g, h)))
                for m in range(NC):
                    last = dve.tensor_tensor_reduce(a_s[:, h % 2, m, :], bk_as[:, m, :], neg[:, m, :], -SCALE, HUGE,
                                                    ALU.add, ALU.min, a_max[:, h % 2, m:m + 1])
                last.then_inc(s_set.sem, 1)

            def a_normalise(g, h):
                dve.wait_ge(p_set.sem, p_set.at(g, h))
                dve.reciprocal(a_inv[:, h % 2], a_sum[:, h % 2]).then_inc(inv_set.sem, 1)

            def a_out(g, _):
                dve.wait_ge(ao_in.sem, ao_in.at(g))
                dve.wait_ge(a_res_set.sem, a_res_set.at(g))
                dve.tensor_tensor(a_y[:], bk_as[:], a_res[:], ALU.add).then_inc(n0.in_ready.sem, 1)
                norm(n0, g, a_y, x1, (near_in, near_in.at(g, -1)), (b_res_set, b_res_set.at(g, -1)))

            def b_near_(g, _):
                dve.wait_ge(near_in.sem, near_in.at(g))
                dve.tensor_copy(b_near[:], bk_b1[:]).then_inc(near_set.sem, 1)

            def b_sum_(g, _):
                dve.wait_ge(yi_in.sem, yi_in.at(g))
                dve.wait_ge(b_res_set.sem, b_res_set.at(g))
                for m in range(NC):
                    last = dve.scalar_tensor_tensor(b_t[:, m, :], bk_b0[:, m, :], deg[:, m:m + 1], b_res[:, m, :],
                                                    ALU.mult, ALU.add)
                last.then_inc(yi_read.sem, 1)
                dve.wait_ge(yi_read.sem, yi_read.at(g))
                dve.wait_ge(yj_in.sem, yj_in.at(g))
                dve.tensor_tensor(b_y[:], bk_b1[:], b_t[:], ALU.add).then_inc(n1.in_ready.sem, 1)
                norm(n1, g, b_y, x2)

            def diagonals(dst, col_of, done):
                for m in range(NC):
                    last = dve.tensor_scalar(dst[:, m, :], ident[:], col_of(m), None, ALU.mult)
                last.then_inc(done.sem, 1)

            def bf(g, _):
                dve.wait_ge(bf_in.sem, bf_in.at(g))
                dve.tensor_copy(b_f[:], bk_b1[:, 0, 0:2 * NC].rearrange("p (m t) -> p m t", t=2)).then_inc(bf_set.sem, 1)
                dve.wait_ge(bf_set.sem, bf_set.at(g))
                diagonals(b_diag, lambda m: b_f[:, m, 1:2], bd_set)

            def gat_scores(filled, masked, src, nf, s, low, nm, slope, s_done, s_at, nm_done):
                wait_apart(dve, masked, filled)
                for m in range(NC):
                    last = dve.tensor_tensor_reduce(s[:, m, :], src, nf[:, m, :], -1.0, HUGE, ALU.add, ALU.min,
                                                    low[:, m:m + 1])
                last.then_inc(s_done.sem, 1)
                dve.wait_ge(s_done.sem, s_at)
                dve.scalar_tensor_tensor(nm[:], low[:], slope, low[:], ALU.mult, ALU.min)
                dve.scalar_tensor_tensor(s[:], s[:], slope, s[:], ALU.mult, ALU.min).then_inc(nm_done.sem, 1)

            def b_scores(g, _):
                gat_scores((bs_in, bs_in.at(g)), (bnf_set, bnf_set.at(g)), bk_b0[:, 0, :], b_nf, b_s, b_min, b_nm,
                           SLOPE2, bs_set, bs_set.at(g), bnm_set)

            def b_turn(g, _):
                dve.wait_ge(bp_set.sem, bp_set.at(g))
                dve.reciprocal(b_inv[:], b_sum[:]).then_inc(binv_set.sem, 1)

            def b_out(g, _):
                dve.wait_ge(bo_in.sem, bo_in.at(g))
                dve.wait_ge(binv_set.sem, binv_set.at(g))
                for m in range(NC):
                    last = dve.scalar_tensor_tensor(b_y2[:, m, :], bk_b1[:, m, :], b_inv[:, m:m + 1], x2[:, m, :],
                                                    ALU.mult, ALU.add)
                last.then_inc(n2.in_ready.sem, 1)
                norm(n2, g, b_y2, x3, (cm_in, cm_in.at(g, -1)), (c_res_set, c_res_set.at(g, -1)))

            def cf(g, _):
                dve.wait_ge(cf_in.sem, cf_in.at(g))
                dve.tensor_copy(c_f[:].rearrange("p m h t -> p (m h t)"), bk_c1[:, 0, 0:2 * NC * H3]).then_inc(cf_set.sem, 1)
                dve.wait_ge(cf_set.sem, cf_set.at(g))
                for h in range(H3):
                    for m in range(NC):
                        last = dve.tensor_scalar(c_diag[:, m, h, :], ident[:], c_f[:, m, h, 1:2], None, ALU.mult)
                last.then_inc(cd_set.sem, 1)

            def c_scores(g, h):
                i = h % 2
                gat_scores((cs_in, cs_in.at(g, h)), (cnf_set, cnf_set.at(g, h)), bk_c0[:, 0, :], c_nf[:, i], c_s[:, i],
                           c_min[:, i], c_nm[:, i], SLOPE3, cs_set, cs_set.at(g, h), cnm_set)

            def c_normalise(g, h):
                dve.wait_ge(cp_set.sem, cp_set.at(g, h))
                dve.reciprocal(c_inv[:, h % 2], c_sum[:, h % 2]).then_inc(cinv_set.sem, 1)

            def c_turn(g, h):
                dve.wait_ge(cpT_in.sem, cpT_in.at(g, h))
                dve.tensor_copy(c_pT[:, h % 2], bk_c1[:]).then_inc(cpT_set.sem, 1)

            def c_head(g, h):
                dve.wait_ge(ce_set.sem, ce_set.at(g, h))
                dve.tensor_scalar(c_e[:, h % 2], c_e[:, h % 2], 1.0, -1.0, ALU.min, ALU.add).then_inc(cg_set.sem, 1)
                dve.wait_ge(cg_set.sem, cg_set.at(g, h))
                dve.tensor_tensor(c_hT[:, h * DC:(h + 1) * DC, :], bk_c2[:], c_e[:, h % 2], ALU.max).then_inc(ch_set.sem, 1)

            def c_join(g, _):
                dve.wait_ge(h2_in.sem, h2_in.at(g))
                dve.tensor_copy(c_h2[:, 0, :], bk_c0[:, :, :].rearrange("p a b -> p (a b)")[:, 0:D + 2]).then_inc(h2a_set.sem, 1)
                dve.wait_ge(h2a_set.sem, h2a_set.at(g))
                dve.wait_ge(h2b_set.sem, h2b_set.at(g))
                diagonals(c_diag5, lambda m: c_h2[:, m, D + 1:D + 2], d5_set)

            def c_scores5(g, _):
                gat_scores((s5_in, s5_in.at(g)), (nf5_set, nf5_set.at(g)), bk_c0[:, 0, :], c_nf5, c_s5, c_min5, c_nm5,
                           SLOPE3, s5_set, s5_set.at(g), nm5_set)

            def c_turn5(g, _):
                dve.wait_ge(p5_set.sem, p5_set.at(g))
                dve.reciprocal(c_inv5[:], c_sum5[:]).then_inc(inv5_set.sem, 1)

            def c_mix5(g, _):
                dve.wait_ge(e5_set.sem, e5_set.at(g))
                dve.tensor_scalar(c_e5[:], c_e5[:], 1.0, -1.0, ALU.min, ALU.add).then_inc(g5_set.sem, 1)
                dve.wait_ge(g5_set.sem, g5_set.at(g))
                for m in range(NC):
                    last = dve.scalar_tensor_tensor(c_o5[:, m, :], bk_c2[:, m, :], c_inv5[:, m:m + 1], c_e5[:, m, :],
                                                    ALU.mult, ALU.max)
                last.then_inc(o5_set.sem, 1)

            def c_ffn2(g, _):
                dve.wait_ge(y_in.sem, y_in.at(g))
                dve.wait_ge(res5_set.sem, res5_set.at(g))
                dve.tensor_tensor(c_y[:], bk_c1[:], c_res5[:], ALU.add).then_inc(n3.in_ready.sem, 1)
                norm(n3, g, c_y, c_n)
                dve.wait_ge(n3.done.sem, n3.done.at(g))
                dve.tensor_tensor(c_ng[:], c_n[:], gammar[:].unsqueeze(1).to_broadcast([P, NC, D]), ALU.mult)\
                    .then_inc(ng_set.sem, 1)
                dve.wait_ge(ng_set.sem, ng_set.at(g))
                dve.wait_ge(c_res_set.sem, c_res_set.at(g))
                dve.tensor_tensor(c_z[:], c_ng[:], c_res[:], ALU.add).then_inc(n4.in_ready.sem, 1)
                norm(n4, g, c_z, c_out, (stored, stored.at(g, -1)))

            def after(fn, setup):
                def step(g, k):
                    fn(g, k)
                    if isinstance(g, int) and g == 0:
                        setup()
                return step

            run(dve, {
                ("a", "q"): aq, ("a", "scores"): a_scores, ("a", "normalise"): a_normalise, ("a", "out"): after(a_out, fold_b),
                ("b", "near"): b_near_, ("b", "sum"): b_sum_, ("b", "f"): bf, ("b", "scores"): b_scores,
                ("b", "turn"): b_turn, ("b", "out"): after(b_out, fold_c),
                ("c", "f"): cf, ("c", "scores"): c_scores, ("c", "normalise"): c_normalise, ("c", "turn"): c_turn,
                ("c", "head"): c_head, ("c", "join"): c_join, ("c", "scores5"): c_scores5, ("c", "turn5"): c_turn5,
                ("c", "mix5"): c_mix5, ("c", "ffn2"): c_ffn2,
            })

        @block.gpsimd
        def _(pool):
            passed[pool] = ctx.enter_context(nc.semaphore("pool_waits_passed"))
            grant(pool, pn_set, cpn_set, b_res_set, c_res_set)
            pool.memset(ident[:], 0.0).then_inc(consts_set.sem, 1)
            pool.memset(ones[:], 1.0).then_inc(consts_set.sem, 1)
            pool.memset(minus_half[:], -0.5).then_inc(consts_set.sem, 1)
            pool.wait_ge(consts_set.sem, 3)
            pool.affine_select(out=ident[:], in_=ident[:], compare_op=ALU.not_equal, fill=1.0, base=0,
                               pattern=[[-1, P]], channel_multiplier=1).then_inc(ident_set.sem, 1)

            def power(n):
                def step(g, _):
                    pool.wait_ge(n.ve_ready.sem, n.ve_ready.at(g))
                    pool.tensor_tensor(n.rstd[:], n.ve[:], minus_half[:], ALU.pow).then_inc(n.rstd_ready.sem, 1)
                return step

            pool.wait_ge(ab_set.sem, 1)

            def ax(g, _):
                pool.wait_ge(x_loaded.sem, x_loaded.at(g))
                pool.wait_ge(n0.in_ready.sem, n0.in_ready.at(g, -1))
                pool.tensor_tensor(a_res[:], a_x[:], attn_bias[:].unsqueeze(1).to_broadcast([P, NC, D]), ALU.add)\
                    .then_inc(a_res_set.sem, 1)

            def divide(p, inv, pn, done):
                for m in range(NC):
                    last = pool.tensor_scalar(pn[:, m, :], p[:, m, :], inv[:, m:m + 1], 1.0, ALU.mult, ALU.mult)
                last.then_inc(done.sem, 1)

            def a_normalise(g, h):
                wait_apart(pool, (inv_set, inv_set.at(g, h)), (pT_in, pT_in.at(g, h - 2)))
                divide(a_p[:, h % 2], a_inv[:, h % 2], a_pn[:, h % 2], pn_set)

            def add_mask(nf, f1, done):
                for m in range(NC):
                    last = pool.tensor_scalar(nf[:, m, :], neg[:, m, :], f1(m), 1.0, ALU.add, ALU.mult)
                last.then_inc(done.sem, 1)

            def bf(g, _):
                wait_apart(pool, (bf_set, bf_set.at(g)))
                add_mask(b_nf, lambda m: b_f[:, m, 0:1], bnf_set)

            def c_mask(g, h):
                wait_apart(pool, (cf_set, cf_set.at(g)), (cs_set, cs_set.at(g, h - 2)))
                add_mask(c_nf[:, h % 2], lambda m: c_f[:, m, h, 0:1], cnf_set)

            def cf(g, _):
                c_mask(g, 0)
                c_mask(g, 1)

            def c_join(g, _):
                wait_apart(pool, (h2a_set, h2a_set.at(g)), (h2b_set, h2b_set.at(g)))
                add_mask(c_nf5, lambda m: c_h2[:, m, D:D + 1], nf5_set)

            def bx(g, _):
                pool.wait_ge(n0.done.sem, n0.done.at(g))
                pool.tensor_tensor(b_res[:], x1[:], deg_bias[:], ALU.add).then_inc(b_res_set.sem, 1)

            def cx(g, _):
                pool.wait_ge(n2.done.sem, n2.done.at(g))
                pool.tensor_tensor(c_res[:], x3[:], betar[:].unsqueeze(1).to_broadcast([P, NC, D]), ALU.add)\
                    .then_inc(c_res_set.sem, 1)

            def c_normalise(g, h):
                wait_apart(pool, (cinv_set, cinv_set.at(g, h)), (cpT_in, cpT_in.at(g, h - 2)))
                divide(c_p[:, h % 2], c_inv[:, h % 2], c_pn[:, h % 2], cpn_set)
                if h + 2 < H3:
                    c_mask(g, h + 2)

            def c_x5(g, _):
                pool.wait_ge(o5_set.sem, o5_set.at(g))
                pool.tensor_tensor(c_res5[:], c_o5[:], bf2r[:].unsqueeze(1).to_broadcast([P, NC, D]), ALU.add)\
                    .then_inc(res5_set.sem, 1)

            def c_ffn2(g, k):
                power(n3)(g, k)
                power(n4)(g, k)

            def once(fn, sig, value):
                def step(g, k):
                    if isinstance(g, int) and g == 0:
                        pool.wait_ge(sig.sem, value)
                    fn(g, k)
                return step

            run(pool, {
                ("a", "x"): ax, ("a", "normalise"): a_normalise, ("a", "out"): power(n0),
                ("b", "x"): once(bx, db_set, 1), ("b", "sum"): power(n1), ("b", "f"): bf, ("b", "out"): power(n2),
                ("c", "x"): once(cx, c_loaded, LOADED["c"]), ("c", "f"): cf, ("c", "normalise"): c_normalise,
                ("c", "join"): c_join, ("c", "x5"): c_x5,
                ("c", "ffn2"): c_ffn2,
            })


_OUTS = [((32, 256, 256), "float32")]


def kernel(**inputs):
    import numpy as np
    import concourse.bacc as bacc
    from concourse.bass_utils import run_bass_kernel_spmd as run_spmd

    nc = bacc.Bacc("TRN2", target_bir_lowering=False, num_devices=1)
    W1 = np.asarray(inputs["L1_gnn_W"])
    D = W1.shape[0]
    columns = lambda a: np.ascontiguousarray(np.asarray(a).reshape(-1, P).T)
    T = lambda a: np.ascontiguousarray(np.asarray(a).T)
    laid = [
        ("x", inputs["x"]), ("adj", inputs["adj"]),
        ("WqT", T(inputs["L0_gnn_Wq"])), ("bq", columns(inputs["L0_gnn_bq"])),
        ("WkT", T(inputs["L0_gnn_Wk"])), ("bk", columns(inputs["L0_gnn_bk"])),
        ("WvT", T(inputs["L0_gnn_Wv"])), ("bv", columns(inputs["L0_gnn_bv"])),
        ("WoT", T(inputs["L0_gnn_Wo"])), ("bo", inputs["L0_gnn_bo"]),
        ("W1iT", T(W1[:, :D])), ("W1jT", T(W1[:, D:])), ("b1", inputs["L1_gnn_b"]),
        ("W2", inputs["L2_gnn_W"]), ("a2_src", inputs["L2_gnn_a_src"]), ("a2_dst", inputs["L2_gnn_a_dst"]),
        ("W3", inputs["L3_gnn_W_heads"]), ("a3", inputs["L3_gnn_a_heads"]),
        ("Wout", inputs["L3_gnn_W_out"]), ("aout", inputs["L3_gnn_a_out"]),
        ("Wf1", inputs["L3_gnn_w1"]), ("bf1", columns(inputs["L3_gnn_b1"])),
        ("Wf2", inputs["L3_gnn_w2"]), ("bf2", inputs["L3_gnn_b2"]),
        ("gamma", inputs["L3_gnn_ln_gamma"]), ("beta", inputs["L3_gnn_ln_beta"]),
    ]
    arrays, args = {}, []
    for name, a in laid:
        a = np.ascontiguousarray(a)
        arrays[f"in_{name}_dram"] = a
        args.append(nc.dram_tensor(f"in_{name}_dram", a.shape, mybir.dt.from_np(a.dtype), kind="ExternalInput").ap())
    for i, (shape, dtype) in enumerate(_OUTS):
        args.append(nc.dram_tensor(f"out_{i}_dram", shape, mybir.dt.from_np(np.dtype(dtype)), kind="ExternalOutput").ap())
    build(nc, *args)
    r = run_spmd(nc, [arrays], core_ids=[0])
    return r.results[0]["out_0_dram"]
```

```python
from contextlib import ExitStack

import concourse.bass as bass
from concourse import mybir

F32 = mybir.dt.float32
F32R = mybir.dt.float32r
I32 = mybir.dt.int32
ALU = mybir.AluOpType
ACT = mybir.ActivationFunctionType
AX_X = mybir.AxisListType.X

P = 128
EPS = 1e-5
MASKED = -1e30
HUGE = 3e38


class Signal:

    def __init__(self, sem, per_graph=1, credit=0, step=1):
        self.sem, self.n, self.credit, self.step = sem, per_graph, credit, step

    def at(self, g, k=None):
        k = self.n - 1 if k is None else k
        return g * (self.n * self.step) + (self.credit + k + 1) * self.step


PLACE = {'a': [1, 7, 11, 18, 36, 37, 38, 41, 42, 43, 47, 48, 49, 51, 52, 53, 55, 57, 58, 59, 60, 63, 64, 65, 66, 68, 69, 70, 71, 72, 73, 77, 80, 1000, 1004, 1005, 1006, 1008], 'b': [1012, 1016, 1022, 1028, 1032, 1035, 1044, 1050, 1061, 1067, 1078, 2003], 'c': [2009, 2010, 2013, 2014, 2015, 2019, 2020, 2021, 2024, 2025, 2026, 2027, 2029, 2030, 2031, 2034, 2039, 2045, 2046, 2054, 2062, 2075, 3002], 'd': [3017, 3023, 3033, 3040, 3056, 3076, 3079, 4074]}


def interleave(streams):
    timed = []
    for name, steps in streams.items():
        assert len(steps) == len(PLACE[name])
        for (s, k), t in zip(steps, PLACE[name]):
            timed.append((t % 1000, t // 1000, name, s, k))
    timed.sort()
    return [(delay, name, s, k) for _, delay, name, s, k in timed]


def attention_steps(load, heads, tail):
    out = list(load)
    for t in range(heads + 3):
        if t < heads:
            out.append(("scores", t))
        if 0 <= t - 1 < heads:
            out.append(("normalise", t - 1))
        if 0 <= t - 2 < heads:
            out.append(("turn", t - 2))
        if 0 <= t - 3 < heads:
            out.append(("mix", t - 3))
    return out + list(tail)


def build(nc, x, adj, Wq, bq, Wk, bk, Wv, bv, Wo, bo, W1i, W1j, b1m, W2, a2s, a2d,
          W3, a3, Wout, aout, Wf1, bf1, Wf2, bf2, gamma, beta, out):
    G, N, D = x.shape
    NC = N // P
    DC = D // P
    H0 = 8
    DH = D // H0
    HG = P // DH
    H3 = W3.shape[0]
    HC = H3 * DC
    SCALE = float(DH) ** -0.5
    SLOPE2, SLOPE3 = 0.2, 0.01

    A = attention_steps([("x", 0), ("q", 0), ("k", 0), ("v", 0)], H0, [("out", 0), ("norm", 0)])
    B = [(s, 0) for s in ("x", "near", "yi", "yj", "norm1", "x2", "f", "scores", "turn", "mix", "out", "norm2")]
    C = attention_steps([("x", 0), ("f", 0)], H3, [])
    C = [s for c in C for s in ([c, ("head", c[1])] if c[0] == "mix" else [c])]
    C += [("join", 0)]
    D5 = [(s, 0) for s in ("scores", "turn", "mix", "x", "ffn1", "ffn2", "norm3", "norm4")]
    ORDER = interleave({"a": A, "b": B, "c": C, "d": D5})
    BEHIND = max(delay for delay, *_ in ORDER)

    def when(stream, what, k=0):
        place = [n for n, step in enumerate(ORDER) if step[1:] == (stream, what, k)][0]
        return ORDER[place][0] * len(ORDER) + place

    assert when("a", "norm") < when("b", "x") and when("b", "near") < when("a", "norm") + len(ORDER)
    assert when("b", "norm2") < when("c", "x") and when("c", "join") < when("b", "norm2") + len(ORDER)
    assert when("c", "join") < when("d", "scores") and when("d", "norm3") < when("c", "join") + len(ORDER)

    with ExitStack() as ctx:
        def sb(name, shape, dt=F32):
            return ctx.enter_context(nc.sbuf_tensor(name, shape, dt))

        def signal(name, per_graph=1, credit=0, step=1):
            return Signal(ctx.enter_context(nc.semaphore(name)), per_graph, credit, step)

        def bank(name):
            return ctx.enter_context(nc.psum_tensor(name, [P, 2, 256], F32))

        bk_at, bk_as, bk_ao = bank("bk_at"), bank("bk_as"), bank("bk_ao")
        bk_b = bank("bk_b")
        bk_cs, bk_ct, bk_cm = bank("bk_cs"), bank("bk_ct"), bank("bk_cm")
        bk_d = bank("bk_d")

        ident, ones = sb("ident", [P, P]), sb("ones", [P, P])
        minus_half = sb("minus_half", [P, NC])
        adjT = sb("adjT", [P, NC, N], F32R)
        neg = sb("neg", [P, NC, N])
        deg = sb("deg", [P, NC])
        wq_h, wk_h, wv_h, wq_l, wk_l, wv_l = (sb(n, [P, DC, D], F32R) for n in
                                              ("wq_h", "wk_h", "wv_h", "wq_l", "wk_l", "wv_l"))
        wo = sb("wo", [P, DC, D])
        bqc, bkc, bvc, bf1c = (sb(n, [P, DC]) for n in ("bqc", "bkc", "bvc", "bf1c"))
        bf2r, gammar, betar = (sb(n, [P, D]) for n in ("bf2r", "gammar", "betar"))
        attn_bias = sb("attn_bias", [P, D])
        deg_bias = sb("deg_bias", [P, NC, D])
        w1i, w1j, w2, wf1, wf2 = (sb(n, [P, DC, D]) for n in ("w1i", "w1j", "w2", "wf1", "wf2"))
        w3 = sb("w3", [P, DC, H3, D])
        w5 = sb("w5", [P, HC, D + 2])
        u2 = sb("u2", [P, DC, 2])
        u3 = sb("u3", [P, DC, H3, 2])

        a_x, a_v, a_res = (sb(n, [P, 2, 256]) for n in ("a_x", "a_v", "a_res"))
        a_xT_h, a_xT_l = sb("a_xT_h", [P, 2, 256], F32R), sb("a_xT_l", [P, 2, 256], F32R)
        a_qh, a_ql, a_kh, a_kl = (sb(n, [P, DC, N], F32R) for n in ("a_qh", "a_ql", "a_kh", "a_kl"))
        a_qs, a_ks = sb("a_qs", [P, H0, N], F32R), sb("a_ks", [P, H0, N], F32R)
        a_s, a_p, a_pT = (sb(n, [P, 2, 2, 256]) for n in ("a_s", "a_p", "a_pT"))
        a_max, a_sum, a_inv = (sb(n, [P, 2, NC]) for n in ("a_max", "a_sum", "a_inv"))
        a_oT = sb("a_oT", [P, 2, 256])
        a_y, x1 = sb("a_y", [P, NC, D]), sb("x1", [P, NC, D])
        x1_h, x1_l = sb("x1_h", [P, NC, D], F32R), sb("x1_l", [P, NC, D], F32R)
        b_xT, b_near, b_res, b_t, b_y, x2, b_x2T = (sb(n, [P, 2, 256]) for n in
                                                    ("b_xT", "b_near", "b_res", "b_t", "b_y", "x2", "b_x2T"))
        b_f, b_diag = sb("b_f", [P, NC, 2]), sb("b_diag", [P, NC, P])
        b_s, b_p, b_pT, b_mix, b_y2, x3 = (sb(n, [P, 2, 256]) for n in
                                                ("b_s", "b_p", "b_pT", "b_mix", "b_y2", "x3"))
        b_nf = sb("b_nf", [P, NC, N])
        b_min, b_nm, b_sum, b_inv = (sb(n, [P, NC]) for n in ("b_min", "b_nm", "b_sum", "b_inv"))
        c_xT, c_res = sb("c_xT", [P, 2, 256]), sb("c_res", [P, NC, D])
        c_f, c_diag = sb("c_f", [P, NC, H3, 2]), sb("c_diag", [P, NC, H3, P])
        c_s, c_p, c_pT, c_mix, c_e = (sb(n, [P, 2, 2, 256]) for n in ("c_s", "c_p", "c_pT", "c_mix", "c_e"))
        c_nf = sb("c_nf", [P, 2, NC, N])
        c_min, c_nm, c_sum, c_inv = (sb(n, [P, 2, NC]) for n in ("c_min", "c_nm", "c_sum", "c_inv"))
        c_hT = sb("c_hT", [P, HC, 256])
        c_h2 = sb("c_h2", [P, NC, D + 2])
        c_diag5 = sb("c_diag5", [P, NC, P])
        c_s5, c_p5, c_pT5, c_e5, c_o5, c_o5T, c_res5, c_hid, c_y, c_n, c_out = (
            sb(n, [P, 2, 256]) for n in ("c_s5", "c_p5", "c_pT5", "c_e5", "c_o5", "c_o5T", "c_res5",
                                         "c_hid", "c_y", "c_n", "c_out"))
        c_nf5 = sb("c_nf5", [P, NC, N])
        c_min5, c_nm5, c_sum5, c_inv5 = (sb(n, [P, NC]) for n in ("c_min5", "c_nm5", "c_sum5", "c_inv5"))

        a3r = c_hT[:].rearrange("p k n -> p (k n)").rearrange("p (h t o) -> p h t o", h=H3, t=2)
        a2r, a5r, scratch, bv_wide = c_s5[:], c_p5[:], c_y[:, 0, :], c_n[:, :, 0:P]
        w_raw = (c_mix[:, 0], c_mix[:, 1], c_e[:, 0])
        adj_i, adj_f, bor, b1r = c_o5T[:].bitcast(I32), c_e5, c_hid[:, 0, :], c_hid[:, 1, :]

        class Norm:

            def __init__(self, name):
                self.stats = sb(f"{name}_stats", [P, NC, 6])
                self.mv = sb(f"{name}_mv", [P, NC, 2])
                self.ve = sb(f"{name}_ve", [P, NC])
                self.rstd = sb(f"{name}_rstd", [P, NC])
                self.in_ready = signal(f"{name}_in_ready", 1, 1)
                self.stats_ready = signal(f"{name}_stats_ready")
                self.mv_ready = signal(f"{name}_mv_ready")
                self.ve_ready = signal(f"{name}_ve_ready")
                self.rstd_ready = signal(f"{name}_rstd_ready")
                self.done = signal(f"{name}_done")

        n0, n1, n2, n3, n4 = (Norm(f"norm{i}") for i in range(5))

        a_loaded, b_loaded, c_loaded = signal("a_loaded"), signal("b_loaded"), signal("c_loaded")
        ident_set, consts_set = signal("ident_set"), signal("consts_set")
        adjf_set, neg_set, bvw_set = signal("adjf_set"), signal("neg_set"), signal("bvw_set")
        adjT_in, adjT_set, ab_in, ab_set = signal("adjT_in"), signal("adjT_set"), signal("ab_in"), signal("ab_set")
        u2_set, u3_set, u5_set, db_set = signal("u2_set"), signal("u3_set"), signal("u5_set"), signal("db_set")
        scr = signal("scratch_written")
        x_loaded = signal("x_loaded", step=16)
        xT_in, xT_set, xT_low_set, q_in, k_in, v_in, v_set = (
            signal(n) for n in ("xT_in", "xT_set", "xT_low_set", "q_in", "k_in", "v_in", "v_set"))
        qh_set, ql_set, kh_set, kl_set = (signal(n) for n in ("qh_set", "ql_set", "kh_set", "kl_set"))
        q_stacked, k_stacked = (signal(n, step=16 * 4 * HG) for n in ("q_stacked", "k_stacked"))
        a_res_set = signal("a_res_set")
        w_high_set, w_low_set = signal("w_high_set"), signal("w_low_set")
        x1_high_set, x1_low_set = signal("x1_high_set"), signal("x1_low_set")
        s_in, p_set, inv_set = (signal(n, H0) for n in ("s_in", "p_set", "inv_set"))
        s_set = signal("s_set", H0, 1)
        pn_set, pT_in, pT_set = (signal(n, H0, 2) for n in ("pn_set", "pT_in", "pT_set"))
        o_in = signal("o_in", H0, 1)
        oT_set, ao_in = signal("oT_set"), signal("ao_in")
        bxT_in, bxT_set, near_in, b_res_set = signal("bxT_in"), signal("bxT_set"), signal("near_in", 1, 1), signal("b_res_set", 1, 1)
        near_set, yi_in, yj_in, yi_read = (signal(n) for n in ("near_set", "yi_in", "yj_in", "yi_read"))
        x2T_in, x2T_set, bf_in, bf_set, bd_set = (signal(n) for n in ("x2T_in", "x2T_set", "bf_in", "bf_set", "bd_set"))
        bs_in, bnf_set, bs_set, bnm_set, bp_set, binv_set = (
            signal(n) for n in ("bs_in", "bnf_set", "bs_set", "bnm_set", "bp_set", "binv_set"))
        bpT_in, bpT_set, bm_in, bm_set, bo_in = (
            signal("bpT_in"), signal("bpT_set"), signal("bm_in"), signal("bm_set"), signal("bo_in"))
        cxT_in, cxT_set, cf_in, cf_set, cd_set, c_res_set = (
            signal("cxT_in"), signal("cxT_set"), signal("cf_in"), signal("cf_set"), signal("cd_set"), signal("c_res_set", 1, 1))
        cs_in, cnf_set, cnm_set, cp_set, cinv_set = (
            signal(n, H3) for n in ("cs_in", "cnf_set", "cnm_set", "cp_set", "cinv_set"))
        cs_set = signal("cs_set", H3, 2)
        cpn_set, cpT_in = signal("cpn_set", H3, 2), signal("cpT_in", H3, 2)
        cpT_set, cm_in, cm_set, ch_in, ce_set, cg_set, ch_set = (
            signal(n, H3, 1 if n in ("cm_in", "cpT_set") else 0) for n in ("cpT_set", "cm_in", "cm_set", "ch_in", "ce_set", "cg_set", "ch_set"))
        h2_in, h2a_set, h2b_set, d5_set = signal("h2_in"), signal("h2a_set"), signal("h2b_set", 1, 1), signal("d5_set")
        s5_in, nf5_set, s5_set, nm5_set, p5_set, inv5_set = (
            signal(n) for n in ("s5_in", "nf5_set", "s5_set", "nm5_set", "p5_set", "inv5_set"))
        pT5_in, pT5_set, m5_in, e5_set, g5_set, o5_set = (
            signal(n) for n in ("pT5_in", "pT5_set", "m5_in", "e5_set", "g5_set", "o5_set"))
        o5T_in, o5T_set, res5_set, hid_in, hid_set, y_in = (
            signal("o5T_in"), signal("o5T_set"), signal("res5_set"), signal("hid_in"), signal("hid_set"),
            signal("y_in"))
        ng_set = signal("ng_set")
        stored = signal("stored", 1, 1, step=16)

        block = ctx.enter_context(nc.Block())

        def run(eng, steps, end=G):
            def iteration(i, whole):
                for delay, stream, what, k in ORDER:
                    if (stream, what) in steps and (whole or 0 <= i - delay < G):
                        steps[stream, what](i - delay, k)

            for i in range(BEHIND):
                iteration(i, False)
            with eng.Fori(BEHIND, end) as i:
                iteration(i, True)
            for i in range(end, G + BEHIND):
                iteration(i, False)

        rows = lambda w: w.rearrange("(c p) o -> p c o", p=P)
        wide = lambda v: v.partition_broadcast(P)

        def graph_rows(t, g):
            return t.rearrange("g (c p) f -> g p c f", p=P)[g]

        def grant(eng, *signals):
            for sig in signals:
                eng.sem_inc(sig.sem, sig.credit * sig.step)

        passed = {}

        def wait_apart(eng, *waits):
            for sig, value in waits:
                eng.wait_ge(sig.sem, value)
            eng.sem_inc(passed[eng], 1)

        @block.sync
        def _(sp):
            grant(sp, stored)
            loads_a = [(adj_i, rows(adj)), (w_raw[0], rows(Wq)), (bqc[:], bq),
                       (w_raw[1], rows(Wk)), (bkc[:], bk), (w_raw[2], rows(Wv)),
                       (wo[:], rows(Wo)), (bvc[:], bv), (bor, wide(bo))]
            loads_b = [(w1i[:], rows(W1i)), (w1j[:], rows(W1j)), (b1r, wide(b1m)), (w2[:], rows(W2)),
                       (a2r[:, 0, :], wide(a2s)), (a2r[:, 1, :], wide(a2d))]
            loads_c = [(w3[:, :, h, :], rows(W3[h])) for h in range(H3)]
            loads_c += [(a3r, wide(a3.rearrange("h (t o) -> h t o", t=2))), (w5[:, :, 0:D], rows(Wout)),
                        (a5r, wide(aout.rearrange("(t o) -> t o", t=2))), (wf1[:], rows(Wf1)), (bf1c[:], bf1),
                        (wf2[:], rows(Wf2)), (bf2r[:], wide(bf2)), (gammar[:], wide(gamma)), (betar[:], wide(beta))]
            sp.dma_start(a_x[:], graph_rows(x, 0)).then_inc(x_loaded.sem, 16)
            for sig, loads in ((a_loaded, loads_a), (b_loaded, loads_b), (c_loaded, loads_c)):
                for dst, src in loads:
                    sp.dma_start(dst, src).then_inc(sig.sem, 16)

            def load_next(g, h):
                if h or (isinstance(g, int) and g == G - 1):
                    return
                sp.wait_ge(xT_in.sem, xT_in.at(g))
                sp.wait_ge(a_res_set.sem, a_res_set.at(g))
                sp.dma_start(a_x[:], graph_rows(x, g + 1)).then_inc(x_loaded.sem, 16)

            def stack(dst, quarters, low_set, stacked):
                def step(g, _):
                    sp.wait_ge(low_set.sem, low_set.at(g))
                    for r, part in enumerate(quarters):
                        for j in range(HG):
                            sp.dma_start(dst[r * DH:(r + 1) * DH, j:H0:HG, :].bitcast(F32),
                                         part[j * DH:(j + 1) * DH, :, :].bitcast(F32)).then_inc(stacked.sem, 16)
                return step

            def store(g, _):
                sp.wait_ge(n4.done.sem, n4.done.at(g))
                sp.dma_start(graph_rows(out, g), c_out[:]).then_inc(stored.sem, 16)

            run(sp, {
                ("a", "q"): stack(a_qs, (a_qh, a_ql, a_qh, a_ql), ql_set, q_stacked),
                ("a", "k"): stack(a_ks, (a_kh, a_kh, a_kl, a_kl), kl_set, k_stacked),
                ("a", "mix"): load_next, ("d", "norm4"): store,
            }, end=G - 1)
            sp.wait_ge(stored.sem, stored.at(G - 1))

        LOADED = {"a": 9 * 16, "b": 6 * 16, "c": (H3 + 9) * 16}

        @block.tensor
        def _(pe):
            def turn(dst, src):
                for r in range(2):
                    for c in range(2):
                        last = pe.transpose(dst[:, c, r * P:(r + 1) * P], src[:, r, c * P:(c + 1) * P], ident[:])
                return last

            def product(dst, lhsT, rhs, chunks=2):
                for m in range(2):
                    for k in range(chunks):
                        last = pe.matmul(dst[:, m, :], lhsT[:, k, m * P:(m + 1) * P], rhs[:, k, :],
                                         start=(k == 0), stop=(k == chunks - 1))
                return last

            def split_product(dst, lhs_parts, rhs_parts):
                pairs = [(a, b) for i, a in enumerate(lhs_parts) for j, b in enumerate(rhs_parts) if i + j < 2]
                for m in range(2):
                    for n, (k, (a, b)) in enumerate((k, pair) for k in range(2) for pair in pairs):
                        last = pe.matmul(dst[:, m, :], a[:, k, m * P:(m + 1) * P], b[:, k, :],
                                         start=(n == 0), stop=(n == 2 * len(pairs) - 1))
                return last

            grant(pe, o_in, near_in, cm_in, pT_in, cpT_in)
            pe.wait_ge(ident_set.sem, 1)
            pe.wait_ge(adjf_set.sem, 1)
            turn(bk_at, adj_f).then_inc(adjT_in.sem, 1)
            pe.wait_ge(bvw_set.sem, 1)
            for k in range(DC):
                last = pe.matmul(bk_as[:, 0, :], bv_wide[:, k, :], wo[:, k, :], start=(k == 0), stop=(k == DC - 1))
            last.then_inc(ab_in.sem, 1)
            pe.wait_ge(a_loaded.sem, LOADED["a"])
            pe.wait_ge(adjT_set.sem, 1)
            pe.wait_ge(ab_set.sem, 1)
            pe.wait_ge(w_low_set.sem, 3)
            pe.wait_ge(consts_set.sem, 2)

            def ax(g, _):
                pe.wait_ge(x_loaded.sem, x_loaded.at(g))
                pe.wait_ge(s_set.sem, s_set.at(g, -1))
                turn(bk_as, a_x).then_inc(xT_in.sem, 1)

            def aq(g, _):
                pe.wait_ge(xT_low_set.sem, xT_low_set.at(g))
                split_product(bk_as, (wq_h, wq_l), (a_xT_h, a_xT_l)).then_inc(q_in.sem, 1)

            def ak(g, _):
                pe.wait_ge(pT_set.sem, pT_set.at(g, -1))
                split_product(bk_at, (wk_h, wk_l), (a_xT_h, a_xT_l)).then_inc(k_in.sem, 1)

            def av(g, _):
                pe.wait_ge(ql_set.sem, ql_set.at(g))
                split_product(bk_as, (a_xT_h, a_xT_l), (wv_h, wv_l)).then_inc(v_in.sem, 1)

            def a_scores(g, h):
                if h == 0:
                    pe.wait_ge(q_stacked.sem, q_stacked.at(g))
                    pe.wait_ge(k_stacked.sem, k_stacked.at(g))
                    pe.wait_ge(v_set.sem, v_set.at(g))
                else:
                    pe.wait_ge(s_set.sem, s_set.at(g, h - 1))
                for m in range(NC):
                    last = pe.matmul(bk_as[:, m, :], a_qs[:, h, m * P:(m + 1) * P], a_ks[:, h, :],
                                     start=True, stop=True)
                last.then_inc(s_in.sem, 1)

            def a_turn(g, h):
                if h > 0:
                    pe.wait_ge(pT_set.sem, pT_set.at(g, h - 1))
                pe.wait_ge(pn_set.sem, pn_set.at(g, h))
                turn(bk_at, a_p[:, h % 2]).then_inc(pT_in.sem, 1)

            def a_mix(g, h):
                if h == 0:
                    pe.wait_ge(n0.in_ready.sem, n0.in_ready.at(g, -1))
                pe.wait_ge(pT_set.sem, pT_set.at(g, h))
                r, c = (h % HG) * DH, h // HG
                for k in range(NC):
                    last = pe.matmul(bk_ao[r:r + DH, c, :], a_v[:, k, h * DH:(h + 1) * DH], a_pT[:, h % 2, k, :],
                                     start=(k == 0), stop=(k == NC - 1))
                last.then_inc(o_in.sem, 1)

            def a_out(g, _):
                pe.wait_ge(oT_set.sem, oT_set.at(g))
                product(bk_ao, a_oT, wo).then_inc(ao_in.sem, 1)

            def bx(g, _):
                pe.wait_ge(n0.done.sem, n0.done.at(g))
                pe.wait_ge(n2.in_ready.sem, n2.in_ready.at(g, -1))
                turn(bk_b, x1).then_inc(bxT_in.sem, 1)

            def b_near_(g, _):
                pe.wait_ge(bxT_set.sem, bxT_set.at(g))
                pe.wait_ge(x1_low_set.sem, x1_low_set.at(g))
                split_product(bk_b, (x1_h, x1_l), (adjT,)).then_inc(near_in.sem, 1)

            def b_yi(g, _):
                pe.wait_ge(near_set.sem, near_set.at(g))
                product(bk_b, b_xT, w1i).then_inc(yi_in.sem, 1)

            def b_yj(g, _):
                pe.wait_ge(yi_read.sem, yi_read.at(g))
                product(bk_b, b_near, w1j).then_inc(yj_in.sem, 1)

            def bx2(g, _):
                pe.wait_ge(n1.done.sem, n1.done.at(g))
                turn(bk_b, x2).then_inc(x2T_in.sem, 1)

            def bf(g, _):
                pe.wait_ge(x2T_set.sem, x2T_set.at(g))
                for m in range(NC):
                    for k in range(DC):
                        last = pe.matmul(bk_b[:, 0, 2 * m:2 * m + 2], b_x2T[:, k, m * P:(m + 1) * P], u2[:, k, :],
                                         start=(k == 0), stop=(k == DC - 1))
                last.then_inc(bf_in.sem, 1)

            def spread(dst, diag):
                for k in range(NC):
                    last = pe.matmul(dst[:, k * P:(k + 1) * P], ones[:], diag[:, k, :], start=True, stop=True)
                return last

            def b_scores(g, _):
                pe.wait_ge(bd_set.sem, bd_set.at(g))
                spread(bk_b[:, 0, :], b_diag).then_inc(bs_in.sem, 1)

            def b_turn(g, _):
                pe.wait_ge(bp_set.sem, bp_set.at(g))
                turn(bk_b, b_p).then_inc(bpT_in.sem, 1)

            def b_mix_(g, _):
                pe.wait_ge(bpT_set.sem, bpT_set.at(g))
                product(bk_b, x2, b_pT).then_inc(bm_in.sem, 1)

            def b_out(g, _):
                pe.wait_ge(bm_set.sem, bm_set.at(g))
                product(bk_b, b_mix, w2).then_inc(bo_in.sem, 1)

            def cx(g, _):
                pe.wait_ge(n2.done.sem, n2.done.at(g))
                pe.wait_ge(cs_set.sem, cs_set.at(g, -1))
                turn(bk_cs, x3).then_inc(cxT_in.sem, 1)

            def cf(g, _):
                pe.wait_ge(cxT_set.sem, cxT_set.at(g))
                pe.wait_ge(cpT_set.sem, cpT_set.at(g, -1))
                w = 2 * H3
                for m in range(NC):
                    for k in range(DC):
                        last = pe.matmul(bk_ct[:, 0, w * m:w * m + w], c_xT[:, k, m * P:(m + 1) * P],
                                         u3[:, k, :, :].rearrange("p h t -> p (h t)"),
                                         start=(k == 0), stop=(k == DC - 1))
                last.then_inc(cf_in.sem, 1)

            def c_scores(g, h):
                if h == 0:
                    pe.wait_ge(cd_set.sem, cd_set.at(g))
                else:
                    pe.wait_ge(cs_set.sem, cs_set.at(g, h - 1))
                spread(bk_cs[:, 0, :], c_diag[:, :, h, :]).then_inc(cs_in.sem, 1)

            def c_turn(g, h):
                if h > 0:
                    pe.wait_ge(cpT_set.sem, cpT_set.at(g, h - 1))
                pe.wait_ge(cpn_set.sem, cpn_set.at(g, h))
                turn(bk_ct, c_p[:, h % 2]).then_inc(cpT_in.sem, 1)

            def c_mix_(g, h):
                if h == 0:
                    pe.wait_ge(h2b_set.sem, h2b_set.at(g, -1))
                else:
                    pe.wait_ge(ch_set.sem, ch_set.at(g, h - 1))
                pe.wait_ge(cpT_set.sem, cpT_set.at(g, h))
                product(bk_cm, x3, c_pT[:, h % 2]).then_inc(cm_in.sem, 1)

            def c_head(g, h):
                pe.wait_ge(cm_set.sem, cm_set.at(g, h))
                product(bk_cm, w3[:, :, h, :], c_mix[:, h % 2]).then_inc(ch_in.sem, 1)

            def c_join(g, _):
                pe.wait_ge(ch_set.sem, ch_set.at(g))
                pe.wait_ge(n3.in_ready.sem, n3.in_ready.at(g, -1))
                for m, dst in enumerate((bk_d, bk_cm)):
                    flat = dst[:, :, :].rearrange("p a b -> p (a b)")[:, 0:D + 2]
                    for k in range(HC):
                        last = pe.matmul(flat, c_hT[:, k, m * P:(m + 1) * P], w5[:, k, :],
                                         start=(k == 0), stop=(k == HC - 1))
                last.then_inc(h2_in.sem, 1)

            def d_scores(g, _):
                pe.wait_ge(d5_set.sem, d5_set.at(g))
                spread(bk_d[:, 0, :], c_diag5).then_inc(s5_in.sem, 1)

            def d_turn(g, _):
                pe.wait_ge(p5_set.sem, p5_set.at(g))
                pe.wait_ge(h2b_set.sem, h2b_set.at(g))
                turn(bk_d, c_p5).then_inc(pT5_in.sem, 1)

            def d_mix(g, _):
                pe.wait_ge(pT5_set.sem, pT5_set.at(g))
                product(bk_d, c_pT5, c_h2[:, :, 0:D]).then_inc(m5_in.sem, 1)

            def d_x(g, _):
                pe.wait_ge(o5_set.sem, o5_set.at(g))
                turn(bk_d, c_o5).then_inc(o5T_in.sem, 1)

            def d_ffn1(g, _):
                pe.wait_ge(o5T_set.sem, o5T_set.at(g))
                product(bk_d, wf1, c_o5T).then_inc(hid_in.sem, 1)

            def d_ffn2(g, _):
                pe.wait_ge(hid_set.sem, hid_set.at(g))
                product(bk_d, c_hid, wf2).then_inc(y_in.sem, 1)

            def once(fn, *waits):
                def step(g, k):
                    if isinstance(g, int) and g == 0 and k == 0:
                        for sig, value in waits:
                            pe.wait_ge(sig.sem, value)
                    fn(g, k)
                return step

            run(pe, {
                ("a", "x"): ax, ("a", "q"): aq, ("a", "k"): ak, ("a", "v"): av, ("a", "scores"): a_scores,
                ("a", "turn"): a_turn, ("a", "mix"): a_mix, ("a", "out"): a_out,
                ("b", "x"): once(bx, (b_loaded, LOADED["b"]), (u2_set, 1)), ("b", "near"): b_near_, ("b", "yi"): b_yi, ("b", "yj"): b_yj,
                ("b", "x2"): bx2, ("b", "f"): bf, ("b", "scores"): b_scores, ("b", "turn"): b_turn, ("b", "mix"): b_mix_,
                ("b", "out"): b_out,
                ("c", "x"): once(cx, (c_loaded, LOADED["c"]), (u3_set, 1), (u5_set, 1)), ("c", "f"): cf,
                ("c", "scores"): c_scores, ("c", "turn"): c_turn, ("c", "mix"): c_mix_, ("c", "head"): c_head,
                ("c", "join"): c_join, ("d", "scores"): d_scores, ("d", "turn"): d_turn, ("d", "mix"): d_mix,
                ("d", "x"): d_x, ("d", "ffn1"): d_ffn1, ("d", "ffn2"): d_ffn2,
            })

        @block.scalar
        def _(act):
            grant(act, pT_set, h2b_set)
            act.wait_ge(adjT_in.sem, 1)
            act.activation(adjT[:], bk_at[:], ACT.Copy).then_inc(adjT_set.sem, 1)
            act.wait_ge(a_loaded.sem, LOADED["a"])
            for w_h, w in zip((wq_h, wk_h, wv_h), w_raw):
                act.activation(w_h[:], w, ACT.Copy).then_inc(w_high_set.sem, 1)

            def copy(dst, src, filled, value, done):
                act.wait_ge(filled.sem, value)
                act.activation(dst, src, ACT.Copy).then_inc(done.sem, 1)

            def ax(g, _):
                copy(a_xT_h[:], bk_as[:], xT_in, xT_in.at(g), xT_set)

            def high(dst, bank, bias, filled, g, done):
                act.wait_ge(filled.sem, filled.at(g))
                for c in range(DC):
                    last = act.activation(dst[:, c, :], bank[:, c, :], ACT.Identity, bias=bias[:, c:c + 1])
                last.then_inc(done.sem, 1)

            def aq(g, _):
                high(a_qh, bk_as, bqc, q_in, g, qh_set)

            def ak(g, _):
                high(a_kh, bk_at, bkc, k_in, g, kh_set)

            def av(g, _):
                act.wait_ge(o_in.sem, o_in.at(g, -1))
                copy(a_v[:], bk_as[:], v_in, v_in.at(g), v_set)

            def a_scores(g, h):
                act.wait_ge(s_set.sem, s_set.at(g, h))
                act.wait_ge(pT_in.sem, pT_in.at(g, h - 2))
                for m in range(NC):
                    last = act.activation(a_p[:, h % 2, m, :], a_s[:, h % 2, m, :], ACT.Exp,
                                          bias=a_max[:, h % 2, m:m + 1], scale=-1.0, accum_out=a_sum[:, h % 2, m:m + 1])
                last.then_inc(p_set.sem, 1)

            def a_turn(g, h):
                copy(a_pT[:, h % 2], bk_at[:], pT_in, pT_in.at(g, h), pT_set)

            def a_out(g, _):
                copy(a_oT[:], bk_ao[:], o_in, o_in.at(g), oT_set)

            def gat_probs(s, p, nm, total, done):
                for m in range(NC):
                    last = act.activation(p[:, m, :], s[:, m, :], ACT.Exp, bias=nm[:, m:m + 1], scale=-1.0,
                                          accum_out=total[:, m:m + 1])
                last.then_inc(done.sem, 1)

            def bx(g, _):
                copy(x1_h[:], x1[:], n0.done, n0.done.at(g), x1_high_set)
                copy(b_xT[:], bk_b[:], bxT_in, bxT_in.at(g), bxT_set)

            def bx2(g, _):
                copy(b_x2T[:], bk_b[:], x2T_in, x2T_in.at(g), x2T_set)

            def b_scores(g, _):
                act.wait_ge(bnm_set.sem, bnm_set.at(g))
                gat_probs(b_s, b_p, b_nm, b_sum, bp_set)

            def b_turn(g, _):
                copy(b_pT[:], bk_b[:], bpT_in, bpT_in.at(g), bpT_set)

            def b_mix_(g, _):
                copy(b_mix[:], bk_b[:], bm_in, bm_in.at(g), bm_set)

            def cx(g, _):
                copy(c_xT[:], bk_cs[:], cxT_in, cxT_in.at(g), cxT_set)

            def c_scores(g, h):
                act.wait_ge(cnm_set.sem, cnm_set.at(g, h))
                act.wait_ge(cpT_in.sem, cpT_in.at(g, h - 2))
                i = h % 2
                gat_probs(c_s[:, i], c_p[:, i], c_nm[:, i], c_sum[:, i], cp_set)

            def c_mix_(g, h):
                copy(c_mix[:, h % 2], bk_cm[:], cm_in, cm_in.at(g, h), cm_set)

            def c_head(g, h):
                act.wait_ge(ch_in.sem, ch_in.at(g, h))
                act.activation(c_e[:, h % 2], bk_cm[:], ACT.Exp).then_inc(ce_set.sem, 1)

            def c_join(g, _):
                act.wait_ge(h2_in.sem, h2_in.at(g))
                act.activation(c_h2[:, 1, :], bk_cm[:, :, :].rearrange("p a b -> p (a b)")[:, 0:D + 2],
                               ACT.Copy).then_inc(h2b_set.sem, 1)

            def d_scores(g, _):
                act.wait_ge(nm5_set.sem, nm5_set.at(g))
                gat_probs(c_s5, c_p5, c_nm5, c_sum5, p5_set)

            def d_turn(g, _):
                copy(c_pT5[:], bk_d[:], pT5_in, pT5_in.at(g), pT5_set)

            def d_mix(g, _):
                act.wait_ge(m5_in.sem, m5_in.at(g))
                act.wait_ge(inv5_set.sem, inv5_set.at(g))
                for m in range(NC):
                    last = act.activation(c_e5[:, m, :], bk_d[:, m, :], ACT.Exp, scale=c_inv5[:, m:m + 1])
                last.then_inc(e5_set.sem, 1)

            def d_x(g, _):
                copy(c_o5T[:], bk_d[:], o5T_in, o5T_in.at(g), o5T_set)

            def d_ffn1(g, _):
                act.wait_ge(hid_in.sem, hid_in.at(g))
                for c in range(DC):
                    last = act.activation(c_hid[:, c, :], bk_d[:, c, :], ACT.Relu, bias=bf1c[:, c:c + 1])
                last.then_inc(hid_set.sem, 1)

            def once(fn, sig, value):
                def step(g, k):
                    if isinstance(g, int) and g == 0:
                        act.wait_ge(sig.sem, value)
                    fn(g, k)
                return step

            run(act, {
                ("a", "x"): ax, ("a", "q"): aq, ("a", "k"): ak, ("a", "v"): av, ("a", "scores"): a_scores, ("a", "turn"): a_turn,
                ("a", "out"): a_out,
                ("b", "x"): bx, ("b", "x2"): bx2, ("b", "scores"): b_scores, ("b", "turn"): b_turn, ("b", "mix"): b_mix_,
                ("c", "x"): once(cx, c_loaded, LOADED["c"]), ("c", "scores"): c_scores, ("c", "mix"): c_mix_,
                ("c", "head"): c_head, ("c", "join"): c_join,
                ("d", "scores"): d_scores, ("d", "turn"): d_turn, ("d", "mix"): d_mix, ("d", "x"): d_x,
                ("d", "ffn1"): d_ffn1,
            })

        @block.vector
        def _(dve):
            passed[dve] = ctx.enter_context(nc.semaphore("vector_waits_passed"))
            grant(dve, n0.in_ready, n1.in_ready, n2.in_ready, n3.in_ready, n4.in_ready, s_set, cs_set, cpT_set)
            dve.wait_ge(a_loaded.sem, LOADED["a"])
            dve.tensor_copy(adj_f[:], adj_i).then_inc(adjf_set.sem, 1)
            dve.wait_ge(adjf_set.sem, 1)
            dve.tensor_scalar(neg[:], adj_f[:], 0.0, MASKED, ALU.is_equal, ALU.mult).then_inc(neg_set.sem, 1)
            dve.tensor_reduce(deg[:], adj_f[:], AX_X, ALU.add).then_inc(neg_set.sem, 1)
            dve.wait_ge(consts_set.sem, 2)
            for k in range(DC):
                last = dve.tensor_scalar(bv_wide[:, k, :], ones[:], bvc[:, k:k + 1], None, ALU.mult)
            last.then_inc(bvw_set.sem, 1)
            dve.wait_ge(ab_in.sem, 1)
            dve.tensor_tensor(attn_bias[:], bk_as[:, 0, :], bor, ALU.add).then_inc(ab_set.sem, 1)
            for n, (w_h, w_l) in enumerate(((wq_h, wq_l), (wk_h, wk_l), (wv_h, wv_l))):
                dve.wait_ge(w_high_set.sem, n + 1)
                dve.tensor_tensor(w_l[:], w_raw[n], w_h[:].bitcast(F32), ALU.subtract)\
                    .then_inc(w_low_set.sem, 1)
            dve.wait_ge(neg_set.sem, 2)
            dve.wait_ge(ident_set.sem, 1)

            written = [0]

            def fold(dst, w, a):
                if written[0]:
                    dve.wait_ge(scr.sem, written[0])
                written[0] += 1
                return dve.tensor_tensor_reduce(scratch, w, a, 1.0, 0.0, ALU.mult, ALU.add, dst)

            def fold_b():
                dve.wait_ge(b_loaded.sem, LOADED["b"])
                for k in range(DC):
                    for t in range(2):
                        fold(u2[:, k, t:t + 1], w2[:, k, :], a2r[:, t, :]).then_inc(scr.sem, 1)
                for m in range(NC):
                    last = dve.tensor_scalar(deg_bias[:, m, :], b1r, deg[:, m:m + 1], None, ALU.mult)
                last.then_inc(db_set.sem, 1)
                dve.wait_ge(scr.sem, written[0])
                dve.sem_inc(u2_set.sem, 1)

            def fold_c():
                dve.wait_ge(c_loaded.sem, LOADED["c"])
                for k in range(DC):
                    for h in range(H3):
                        for t in range(2):
                            fold(u3[:, k, h, t:t + 1], w3[:, k, h, :], a3r[:, h, t, :]).then_inc(scr.sem, 1)
                for k in range(HC):
                    for t in range(2):
                        fold(w5[:, k, D + t:D + t + 1], w5[:, k, 0:D], a5r[:, t, :]).then_inc(scr.sem, 1)
                dve.wait_ge(scr.sem, written[0])
                dve.sem_inc(u3_set.sem, 1)
                dve.sem_inc(u5_set.sem, 1)

            def norm_stats(n, g, src):
                dve.wait_ge(n.in_ready.sem, n.in_ready.at(g))
                for m in range(NC):
                    last = dve.bn_stats(n.stats[:, m, :], src[:, m, :])
                last.then_inc(n.stats_ready.sem, 1)
                wait_apart(dve, (n.stats_ready, n.stats_ready.at(g)))
                for m in range(NC):
                    last = dve.bn_aggr(n.mv[:, m, :], n.stats[:, m, :])
                last.then_inc(n.mv_ready.sem, 1)
                dve.wait_ge(n.mv_ready.sem, n.mv_ready.at(g))
                dve.tensor_scalar(n.ve[:], n.mv[:, :, 1], EPS, None, ALU.add).then_inc(n.ve_ready.sem, 1)

            def norm_apply(n, g, src, dst, *free):
                dve.wait_ge(n.rstd_ready.sem, n.rstd_ready.at(g))
                for sig, value in free:
                    dve.wait_ge(sig.sem, value)
                for m in range(NC):
                    last = dve.tensor_scalar(dst[:, m, :], src[:, m, :], n.mv[:, m, 0:1], n.rstd[:, m:m + 1],
                                             ALU.subtract, ALU.mult)
                last.then_inc(n.done.sem, 1)

            def low(dst, bank, bias, high, high_set, g, done):
                dve.wait_ge(high_set.sem, high_set.at(g))
                for c in range(DC):
                    last = dve.scalar_tensor_tensor(dst[:, c, :], bank[:, c, :], bias[:, c:c + 1],
                                                    high[:, c, :].bitcast(F32), ALU.add, ALU.subtract)
                last.then_inc(done.sem, 1)

            def ax(g, _):
                dve.wait_ge(xT_set.sem, xT_set.at(g))
                dve.tensor_tensor(a_xT_l[:], bk_as[:], a_xT_h[:].bitcast(F32), ALU.subtract).then_inc(xT_low_set.sem, 1)

            def aq(g, _):
                low(a_ql, bk_as, bqc, a_qh, qh_set, g, ql_set)

            def ak(g, _):
                low(a_kl, bk_at, bkc, a_kh, kh_set, g, kl_set)

            def a_scores(g, h):
                wait_apart(dve, (s_in, s_in.at(g, h)))
                for m in range(NC):
                    last = dve.tensor_tensor_reduce(a_s[:, h % 2, m, :], bk_as[:, m, :], neg[:, m, :], -SCALE, HUGE,
                                                    ALU.add, ALU.min, a_max[:, h % 2, m:m + 1])
                last.then_inc(s_set.sem, 1)

            def a_normalise(g, h):
                dve.wait_ge(p_set.sem, p_set.at(g, h))
                dve.reciprocal(a_inv[:, h % 2], a_sum[:, h % 2]).then_inc(inv_set.sem, 1)

            def a_out(g, _):
                dve.wait_ge(ao_in.sem, ao_in.at(g))
                dve.wait_ge(a_res_set.sem, a_res_set.at(g))
                dve.tensor_tensor(a_y[:], bk_ao[:], a_res[:], ALU.add).then_inc(n0.in_ready.sem, 1)
                norm_stats(n0, g, a_y)

            def a_norm(g, _):
                norm_apply(n0, g, a_y, x1, (near_in, near_in.at(g, -1)), (b_res_set, b_res_set.at(g, -1)))

            def b_near_(g, _):
                dve.wait_ge(near_in.sem, near_in.at(g))
                dve.tensor_copy(b_near[:], bk_b[:]).then_inc(near_set.sem, 1)

            def b_yi(g, _):
                dve.wait_ge(yi_in.sem, yi_in.at(g))
                dve.wait_ge(b_res_set.sem, b_res_set.at(g))
                for m in range(NC):
                    last = dve.scalar_tensor_tensor(b_t[:, m, :], bk_b[:, m, :], deg[:, m:m + 1], b_res[:, m, :],
                                                    ALU.mult, ALU.add)
                last.then_inc(yi_read.sem, 1)

            def b_yj(g, _):
                dve.wait_ge(yi_read.sem, yi_read.at(g))
                dve.wait_ge(yj_in.sem, yj_in.at(g))
                dve.tensor_tensor(b_y[:], bk_b[:], b_t[:], ALU.add).then_inc(n1.in_ready.sem, 1)
                norm_stats(n1, g, b_y)

            def b_norm1(g, _):
                norm_apply(n1, g, b_y, x2)

            def diagonals(dst, col_of, done):
                for m in range(NC):
                    last = dve.tensor_scalar(dst[:, m, :], ident[:], col_of(m), None, ALU.mult)
                last.then_inc(done.sem, 1)

            def bf(g, _):
                dve.wait_ge(bf_in.sem, bf_in.at(g))
                dve.tensor_copy(b_f[:], bk_b[:, 0, 0:2 * NC].rearrange("p (m t) -> p m t", t=2)).then_inc(bf_set.sem, 1)
                dve.wait_ge(bf_set.sem, bf_set.at(g))
                diagonals(b_diag, lambda m: b_f[:, m, 1:2], bd_set)

            def gat_scores(filled, masked, src, nf, s, low, nm, slope, s_done, s_at, nm_done):
                wait_apart(dve, masked, filled)
                for m in range(NC):
                    last = dve.tensor_tensor_reduce(s[:, m, :], src, nf[:, m, :], -1.0, HUGE, ALU.add, ALU.min,
                                                    low[:, m:m + 1])
                last.then_inc(s_done.sem, 1)
                dve.wait_ge(s_done.sem, s_at)
                dve.scalar_tensor_tensor(nm[:], low[:], slope, low[:], ALU.mult, ALU.min)
                dve.scalar_tensor_tensor(s[:], s[:], slope, s[:], ALU.mult, ALU.min).then_inc(nm_done.sem, 1)

            def b_scores(g, _):
                gat_scores((bs_in, bs_in.at(g)), (bnf_set, bnf_set.at(g)), bk_b[:, 0, :], b_nf, b_s, b_min, b_nm,
                           SLOPE2, bs_set, bs_set.at(g), bnm_set)

            def b_turn(g, _):
                dve.wait_ge(bp_set.sem, bp_set.at(g))
                dve.reciprocal(b_inv[:], b_sum[:]).then_inc(binv_set.sem, 1)

            def b_out(g, _):
                dve.wait_ge(bo_in.sem, bo_in.at(g))
                dve.wait_ge(binv_set.sem, binv_set.at(g))
                for m in range(NC):
                    last = dve.scalar_tensor_tensor(b_y2[:, m, :], bk_b[:, m, :], b_inv[:, m:m + 1], x2[:, m, :],
                                                    ALU.mult, ALU.add)
                last.then_inc(n2.in_ready.sem, 1)
                norm_stats(n2, g, b_y2)

            def b_norm2(g, _):
                norm_apply(n2, g, b_y2, x3, (cm_in, cm_in.at(g, -1)), (c_res_set, c_res_set.at(g, -1)))

            def cf(g, _):
                dve.wait_ge(cf_in.sem, cf_in.at(g))
                dve.tensor_copy(c_f[:].rearrange("p m h t -> p (m h t)"), bk_ct[:, 0, 0:2 * NC * H3]).then_inc(cf_set.sem, 1)
                dve.wait_ge(cf_set.sem, cf_set.at(g))
                for h in range(H3):
                    for m in range(NC):
                        last = dve.tensor_scalar(c_diag[:, m, h, :], ident[:], c_f[:, m, h, 1:2], None, ALU.mult)
                last.then_inc(cd_set.sem, 1)

            def c_scores(g, h):
                i = h % 2
                gat_scores((cs_in, cs_in.at(g, h)), (cnf_set, cnf_set.at(g, h)), bk_cs[:, 0, :], c_nf[:, i], c_s[:, i],
                           c_min[:, i], c_nm[:, i], SLOPE3, cs_set, cs_set.at(g, h), cnm_set)

            def c_normalise(g, h):
                dve.wait_ge(cp_set.sem, cp_set.at(g, h))
                dve.reciprocal(c_inv[:, h % 2], c_sum[:, h % 2]).then_inc(cinv_set.sem, 1)

            def c_turn(g, h):
                dve.wait_ge(cpT_in.sem, cpT_in.at(g, h))
                dve.tensor_copy(c_pT[:, h % 2], bk_ct[:]).then_inc(cpT_set.sem, 1)

            def c_head(g, h):
                dve.wait_ge(ce_set.sem, ce_set.at(g, h))
                dve.tensor_scalar(c_e[:, h % 2], c_e[:, h % 2], 1.0, -1.0, ALU.min, ALU.add).then_inc(cg_set.sem, 1)
                dve.wait_ge(cg_set.sem, cg_set.at(g, h))
                dve.tensor_tensor(c_hT[:, h * DC:(h + 1) * DC, :], bk_cm[:], c_e[:, h % 2], ALU.max).then_inc(ch_set.sem, 1)

            def c_join(g, _):
                dve.wait_ge(h2_in.sem, h2_in.at(g))
                dve.tensor_copy(c_h2[:, 0, :], bk_d[:, :, :].rearrange("p a b -> p (a b)")[:, 0:D + 2]).then_inc(h2a_set.sem, 1)
                dve.wait_ge(h2a_set.sem, h2a_set.at(g))
                dve.wait_ge(h2b_set.sem, h2b_set.at(g))
                diagonals(c_diag5, lambda m: c_h2[:, m, D + 1:D + 2], d5_set)

            def d_scores(g, _):
                gat_scores((s5_in, s5_in.at(g)), (nf5_set, nf5_set.at(g)), bk_d[:, 0, :], c_nf5, c_s5, c_min5, c_nm5,
                           SLOPE3, s5_set, s5_set.at(g), nm5_set)

            def d_turn(g, _):
                dve.wait_ge(p5_set.sem, p5_set.at(g))
                dve.reciprocal(c_inv5[:], c_sum5[:]).then_inc(inv5_set.sem, 1)

            def d_mix(g, _):
                dve.wait_ge(e5_set.sem, e5_set.at(g))
                dve.tensor_scalar(c_e5[:], c_e5[:], 1.0, -1.0, ALU.min, ALU.add).then_inc(g5_set.sem, 1)
                dve.wait_ge(g5_set.sem, g5_set.at(g))
                for m in range(NC):
                    last = dve.scalar_tensor_tensor(c_o5[:, m, :], bk_d[:, m, :], c_inv5[:, m:m + 1], c_e5[:, m, :],
                                                    ALU.mult, ALU.max)
                last.then_inc(o5_set.sem, 1)

            def d_ffn2(g, _):
                dve.wait_ge(y_in.sem, y_in.at(g))
                dve.wait_ge(res5_set.sem, res5_set.at(g))
                dve.tensor_tensor(c_y[:], bk_d[:], c_res5[:], ALU.add).then_inc(n3.in_ready.sem, 1)
                norm_stats(n3, g, c_y)

            def d_norm3(g, _):
                norm_apply(n3, g, c_y, c_n)
                dve.wait_ge(n3.done.sem, n3.done.at(g))
                dve.tensor_tensor(c_n[:], c_n[:], gammar[:].unsqueeze(1).to_broadcast([P, NC, D]), ALU.mult)\
                    .then_inc(ng_set.sem, 1)
                dve.wait_ge(ng_set.sem, ng_set.at(g))
                dve.wait_ge(c_res_set.sem, c_res_set.at(g))
                dve.tensor_tensor(c_n[:], c_n[:], c_res[:], ALU.add).then_inc(n4.in_ready.sem, 1)
                norm_stats(n4, g, c_n)

            def d_norm4(g, _):
                norm_apply(n4, g, c_n, c_out, (stored, stored.at(g, -1)))

            def after(fn, setup):
                def step(g, k):
                    fn(g, k)
                    if isinstance(g, int) and g == 0:
                        setup()
                return step

            run(dve, {
                ("a", "x"): ax,
                ("a", "q"): aq, ("a", "k"): ak, ("a", "scores"): a_scores, ("a", "normalise"): a_normalise,
                ("a", "out"): a_out, ("a", "norm"): after(a_norm, fold_b),
                ("b", "near"): b_near_, ("b", "yi"): b_yi, ("b", "yj"): b_yj, ("b", "f"): bf, ("b", "scores"): b_scores,
                ("b", "turn"): b_turn, ("b", "out"): b_out, ("b", "norm1"): b_norm1, ("b", "norm2"): after(b_norm2, fold_c),
                ("c", "f"): cf, ("c", "scores"): c_scores, ("c", "normalise"): c_normalise, ("c", "turn"): c_turn,
                ("c", "head"): c_head, ("c", "join"): c_join, ("d", "scores"): d_scores, ("d", "turn"): d_turn,
                ("d", "mix"): d_mix, ("d", "ffn2"): d_ffn2, ("d", "norm3"): d_norm3, ("d", "norm4"): d_norm4,
            })

        @block.gpsimd
        def _(pool):
            passed[pool] = ctx.enter_context(nc.semaphore("pool_waits_passed"))
            grant(pool, pn_set, cpn_set, b_res_set, c_res_set)
            pool.memset(ident[:], 0.0).then_inc(consts_set.sem, 1)
            pool.memset(ones[:], 1.0).then_inc(consts_set.sem, 1)
            pool.memset(minus_half[:], -0.5).then_inc(consts_set.sem, 1)
            pool.wait_ge(consts_set.sem, 3)
            pool.affine_select(out=ident[:], in_=ident[:], compare_op=ALU.not_equal, fill=1.0, base=0,
                               pattern=[[-1, P]], channel_multiplier=1).then_inc(ident_set.sem, 1)

            def power(n):
                def step(g, _):
                    pool.wait_ge(n.ve_ready.sem, n.ve_ready.at(g))
                    pool.tensor_tensor(n.rstd[:], n.ve[:], minus_half[:], ALU.pow).then_inc(n.rstd_ready.sem, 1)
                return step

            pool.wait_ge(ab_set.sem, 1)

            def a_mix(g, h):
                if h:
                    return
                pool.wait_ge(x_loaded.sem, x_loaded.at(g))
                pool.wait_ge(n0.in_ready.sem, n0.in_ready.at(g, -1))
                pool.tensor_tensor(a_res[:], a_x[:], attn_bias[:].unsqueeze(1).to_broadcast([P, NC, D]), ALU.add)\
                    .then_inc(a_res_set.sem, 1)

            def divide(p, inv, done):
                for m in range(NC):
                    last = pool.tensor_scalar(p[:, m, :], p[:, m, :], inv[:, m:m + 1], 1.0, ALU.mult, ALU.mult)
                last.then_inc(done.sem, 1)

            def a_normalise(g, h):
                wait_apart(pool, (inv_set, inv_set.at(g, h)))
                divide(a_p[:, h % 2], a_inv[:, h % 2], pn_set)

            def add_mask(nf, f1, done):
                for m in range(NC):
                    last = pool.tensor_scalar(nf[:, m, :], neg[:, m, :], f1(m), 1.0, ALU.add, ALU.mult)
                last.then_inc(done.sem, 1)

            def bf(g, _):
                wait_apart(pool, (bf_set, bf_set.at(g)))
                add_mask(b_nf, lambda m: b_f[:, m, 0:1], bnf_set)

            def c_mask(g, h):
                wait_apart(pool, (cf_set, cf_set.at(g)), (cs_set, cs_set.at(g, h - 2)))
                add_mask(c_nf[:, h % 2], lambda m: c_f[:, m, h, 0:1], cnf_set)

            def cf(g, _):
                c_mask(g, 0)
                c_mask(g, 1)

            def c_join(g, _):
                c_residual(g)
                wait_apart(pool, (h2a_set, h2a_set.at(g)), (h2b_set, h2b_set.at(g)))
                add_mask(c_nf5, lambda m: c_h2[:, m, D:D + 1], nf5_set)

            def bx(g, _):
                pool.wait_ge(x1_high_set.sem, x1_high_set.at(g))
                pool.tensor_tensor(x1_l[:], x1[:], x1_h[:].bitcast(F32), ALU.subtract).then_inc(x1_low_set.sem, 1)
                pool.tensor_tensor(b_res[:], x1[:], deg_bias[:], ALU.add).then_inc(b_res_set.sem, 1)

            def c_residual(g):
                pool.wait_ge(n2.done.sem, n2.done.at(g))
                pool.wait_ge(n4.in_ready.sem, n4.in_ready.at(g, -1))
                pool.tensor_tensor(c_res[:], x3[:], betar[:].unsqueeze(1).to_broadcast([P, NC, D]), ALU.add)\
                    .then_inc(c_res_set.sem, 1)

            def c_normalise(g, h):
                wait_apart(pool, (cinv_set, cinv_set.at(g, h)))
                divide(c_p[:, h % 2], c_inv[:, h % 2], cpn_set)
                if h + 2 < H3:
                    c_mask(g, h + 2)

            def d_x(g, _):
                pool.wait_ge(o5_set.sem, o5_set.at(g))
                pool.tensor_tensor(c_res5[:], c_o5[:], bf2r[:].unsqueeze(1).to_broadcast([P, NC, D]), ALU.add)\
                    .then_inc(res5_set.sem, 1)

            def once(fn, sig, value):
                def step(g, k):
                    if isinstance(g, int) and g == 0:
                        pool.wait_ge(sig.sem, value)
                    fn(g, k)
                return step

            run(pool, {
                ("a", "mix"): a_mix, ("a", "normalise"): a_normalise, ("a", "out"): power(n0),
                ("b", "x"): once(bx, db_set, 1), ("b", "yj"): power(n1), ("b", "f"): bf, ("b", "out"): power(n2),
                ("c", "f"): cf, ("c", "normalise"): c_normalise,
                ("c", "join"): once(c_join, c_loaded, LOADED["c"]), ("d", "x"): d_x,
                ("d", "ffn2"): power(n3), ("d", "norm3"): power(n4),
            })


_OUTS = [((32, 256, 256), "float32")]


def kernel(**inputs):
    import numpy as np
    import concourse.bacc as bacc
    from concourse.bass_utils import run_bass_kernel_spmd as run_spmd

    nc = bacc.Bacc("TRN2", target_bir_lowering=False, num_devices=1)
    W1 = np.asarray(inputs["L1_gnn_W"])
    D = W1.shape[0]
    columns = lambda a: np.ascontiguousarray(np.asarray(a).reshape(-1, P).T)
    T = lambda a: np.ascontiguousarray(np.asarray(a).T)
    laid = [
        ("x", inputs["x"]), ("adj", inputs["adj"]),
        ("WqT", T(inputs["L0_gnn_Wq"])), ("bq", columns(inputs["L0_gnn_bq"])),
        ("WkT", T(inputs["L0_gnn_Wk"])), ("bk", columns(inputs["L0_gnn_bk"])),
        ("WvT", T(inputs["L0_gnn_Wv"])), ("bv", columns(inputs["L0_gnn_bv"])),
        ("WoT", T(inputs["L0_gnn_Wo"])), ("bo", inputs["L0_gnn_bo"]),
        ("W1iT", T(W1[:, :D])), ("W1jT", T(W1[:, D:])), ("b1", inputs["L1_gnn_b"]),
        ("W2", inputs["L2_gnn_W"]), ("a2_src", inputs["L2_gnn_a_src"]), ("a2_dst", inputs["L2_gnn_a_dst"]),
        ("W3", inputs["L3_gnn_W_heads"]), ("a3", inputs["L3_gnn_a_heads"]),
        ("Wout", inputs["L3_gnn_W_out"]), ("aout", inputs["L3_gnn_a_out"]),
        ("Wf1", inputs["L3_gnn_w1"]), ("bf1", columns(inputs["L3_gnn_b1"])),
        ("Wf2", inputs["L3_gnn_w2"]), ("bf2", inputs["L3_gnn_b2"]),
        ("gamma", inputs["L3_gnn_ln_gamma"]), ("beta", inputs["L3_gnn_ln_beta"]),
    ]
    arrays, args = {}, []
    for name, a in laid:
        a = np.ascontiguousarray(a)
        arrays[f"in_{name}_dram"] = a
        args.append(nc.dram_tensor(f"in_{name}_dram", a.shape, mybir.dt.from_np(a.dtype), kind="ExternalInput").ap())
    for i, (shape, dtype) in enumerate(_OUTS):
        args.append(nc.dram_tensor(f"out_{i}_dram", shape, mybir.dt.from_np(np.dtype(dtype)), kind="ExternalOutput").ap())
    build(nc, *args)
    r = run_spmd(nc, [arrays], core_ids=[0])
    return r.results[0]["out_0_dram"]
```

```python
from contextlib import ExitStack

import concourse.bass as bass
from concourse import mybir

F32 = mybir.dt.float32
F32R = mybir.dt.float32r
I32 = mybir.dt.int32
ALU = mybir.AluOpType
ACT = mybir.ActivationFunctionType
AX_X = mybir.AxisListType.X

P = 128
EPS = 1e-5
MASKED = -1e30
HUGE = 3e38
PE, DVE, SCALAR, POOL, SYNC = range(5)


class Signal:

    def __init__(self, sem, per_graph=1, credit=0, step=1):
        self.sem, self.n, self.credit, self.step = sem, per_graph, credit, step

    def at(self, g, k=None):
        k = self.n - 1 if k is None else k
        return g * (self.n * self.step) + (self.credit + k + 1) * self.step


TABLE = {
    "a": [
        ("x", 0,    3,    3,    5, None, None),
        ("q", 0,    7,    7,   10, None,    0),
        ("k", 0,   11,   12,   17, None,    1),
        ("v", 0,   22, None,   22, None, None),
        ("scores", 0,   25,   20,   25, None, None),
        ("scores", 1,   28,   24,   28, None, None),
        ("normalise", 0, None,   25, None,    4, None),
        ("scores", 2,   30,   27,   30, None, None),
        ("normalise", 1, None,   30, None,    5, None),
        ("turn", 0,   33, None,   32, None, None),
        ("scores", 3,   34,   33,   35, None, None),
        ("normalise", 2, None,   34, None,    7, None),
        ("turn", 1,   38, None,   36, None, None),
        ("mix", 0,   39, None, None,    9,    3),
        ("scores", 4,   40,   39,   40, None, None),
        ("normalise", 3, None,   40, None,   10, None),
        ("turn", 2,   44, None,   42, None, None),
        ("mix", 1,   45, None, None, None, None),
        ("scores", 5,   48,   43,   47, None, None),
        ("normalise", 4, None,   44, None,   12, None),
        ("turn", 3,   52, None,   48, None, None),
        ("mix", 2,   53, None, None, None, None),
        ("scores", 6,   55,   51,  100, None, None),
        ("normalise", 5, None,   53, None,   15, None),
        ("turn", 4,   58, None,  101, None, None),
        ("mix", 3,   59, None, None, None, None),
        ("scores", 7,   60,   57,  104, None, None),
        ("normalise", 6, None,  101, None,   18, None),
        ("turn", 5,  100, None,  106, None, None),
        ("mix", 4,  101, None, None, None, None),
        ("normalise", 7, None,  102, None,   19, None),
        ("turn", 6,  106, None,  109, None, None),
        ("mix", 5,  108, None, None, None, None),
        ("turn", 7,  109, None,  111, None, None),
        ("mix", 6,  112, None, None, None, None),
        ("mix", 7,  113, None, None, None, None),
        ("out", 0,  118,  114,  115,   21, None),
        ("norm", 0, None,  115, None, None, None),
    ],
    "b": [
        ("x", 0,  121, None,  120,   22, None),
        ("near", 0,  123,  121,  124, None, None),
        ("yi", 0,  129,  126, None, None, None),
        ("yj", 0,  141,  148, None,  113, None),
        ("norm1", 0, None,  152, None, None, None),
        ("x2", 0, None, None, None, None, None),
        ("f", 0, None,  156,  203,  116, None),
        ("scores", 0,  204,  206,  213, None, None),
        ("turn", 0,  214,  210,  214, None, None),
        ("mix", 0,  216, None,  218, None, None),
        ("out", 0,  219,  216, None,  123, None),
        ("norm2", 0, None,  219, None, None, None),
    ],
    "c": [
        ("x", 0,  224, None,  223,  201, None),
        ("f", 0,  227,  222,  226,  203, None),
        ("scores", 0,  231,  228,  231, None, None),
        ("scores", 1,  235,  231,  234, None, None),
        ("normalise", 0, None,  232, None,  206, None),
        ("scores", 2,  237,  237,  238, None, None),
        ("normalise", 1, None,  238, None,  208, None),
        ("turn", 0,  243,  241,  239, None, None),
        ("scores", 3,  246,  242,  243, None, None),
        ("normalise", 2, None,  245, None,  211, None),
        ("turn", 1,  249,  246,  244, None, None),
        ("mix", 0,  250,  247,  245, None, None),
        ("head", 0,  254,  249,  246, None, None),
        ("normalise", 3, None,  250, None,  214, None),
        ("turn", 2,  256,  254,  249, None, None),
        ("mix", 1,  257,  255,  250, None, None),
        ("head", 1,  261,  300,  302, None, None),
        ("turn", 3,  302,  304,  307, None, None),
        ("mix", 2,  305,  305,  308, None, None),
        ("head", 2,  310,  308,  312, None, None),
        ("mix", 3,  315,  309,  316, None, None),
        ("head", 3,  317,  313,  319, None, None),
        ("join", 0,  320,  318,  321,  300, None),
    ],
    "d": [
        ("scores", 0,  326,  323,  327, None, None),
        ("turn", 0,  332,  329,  329, None, None),
        ("mix", 0,  336,  336,  333, None, None),
        ("x", 0,  342, None,  337,  317, None),
        ("ffn1", 0,  347, None,  341, None, None),
        ("ffn2", 0,  351,  411, None,  320, None),
        ("norm3", 0, None,  417, None,  402, None),
        ("norm4", 0, None,  435, None, None,  402),
    ],
}


def order(engine):
    timed = sorted((place[engine] % 100, place[engine] // 100, stream, what, k)
                   for stream, steps in TABLE.items() for what, k, *place in steps if place[engine] is not None)
    return [(behind, stream, what, k) for _, behind, stream, what, k in timed]


def build(nc, x, adj, Wq, bq, Wk, bk, Wv, bv, Wo, bo, W1i, W1j, b1m, W2, a2s, a2d,
          W3, a3, Wout, aout, Wf1, bf1, Wf2, bf2, gamma, beta, out):
    G, N, D = x.shape
    NC = N // P
    DC = D // P
    H0 = 8
    DH = D // H0
    HG = P // DH
    H3 = W3.shape[0]
    HC = H3 * DC
    SCALE = float(DH) ** -0.5
    SLOPE2, SLOPE3 = 0.2, 0.01

    ORDERS = [order(engine) for engine in range(5)]
    BEHIND = max(behind for steps in ORDERS for behind, *_ in steps)

    def overtaken(engine, early, late):
        places = {what: place[engine] for what, _, *place in TABLE["d"]}
        return places[early] + 100 <= places[late]

    assert not overtaken(DVE, "mix", "norm4") and not overtaken(DVE, "scores", "norm3")
    assert not overtaken(DVE, "turn", "ffn2")
    assert not overtaken(PE, "turn", "ffn2") and not overtaken(PE, "scores", "ffn1")

    with ExitStack() as ctx:
        def sb(name, shape, dt=F32):
            return ctx.enter_context(nc.sbuf_tensor(name, shape, dt))

        def signal(name, per_graph=1, credit=0, step=1):
            return Signal(ctx.enter_context(nc.semaphore(name)), per_graph, credit, step)

        def bank(name):
            return ctx.enter_context(nc.psum_tensor(name, [P, 2, 256], F32))

        bk_at, bk_as, bk_ao = bank("bk_at"), bank("bk_as"), bank("bk_ao")
        bk_b = bank("bk_b")
        bk_cs, bk_ct, bk_cm = bank("bk_cs"), bank("bk_ct"), bank("bk_cm")
        bk_d = bank("bk_d")

        ident, ones = sb("ident", [P, P]), sb("ones", [P, P])
        minus_half = sb("minus_half", [P, NC])
        adjT = sb("adjT", [P, NC, N], F32R)
        neg = sb("neg", [P, NC, N])
        deg = sb("deg", [P, NC])
        wq_h, wk_h, wv_h, w1j_h, wq_l, wk_l, wv_l, w1j_l = (sb(n, [P, DC, D], F32R) for n in
                                              ("wq_h", "wk_h", "wv_h", "w1j_h", "wq_l", "wk_l", "wv_l", "w1j_l"))
        wo = sb("wo", [P, DC, D])
        bqc, bkc, bvc, bf1c = (sb(n, [P, DC]) for n in ("bqc", "bkc", "bvc", "bf1c"))
        bf2r, gammar, betar = (sb(n, [P, D]) for n in ("bf2r", "gammar", "betar"))
        attn_bias = sb("attn_bias", [P, D])
        deg_bias = sb("deg_bias", [P, NC, D])
        w1i, w2, wf1, wf2 = (sb(n, [P, DC, D]) for n in ("w1i", "w2", "wf1", "wf2"))
        w3_h, w3_l = sb("w3_h", [P, DC, H3, D], F32R), sb("w3_l", [P, DC, H3, D], F32R)
        w5 = sb("w5", [P, HC, D + 2])
        u2, u2_rows = sb("u2", [P, DC, 2]), sb("u2_rows", [P, 2, D])
        u3 = sb("u3", [P, DC, H3, 2])

        a_x, a_v, a_res = (sb(n, [P, 2, 256]) for n in ("a_x", "a_v", "a_res"))
        a_xT_h, a_xT_l = sb("a_xT_h", [P, 2, 256], F32R), sb("a_xT_l", [P, 2, 256], F32R)
        a_qh, a_ql, a_kh, a_kl = (sb(n, [P, DC, N], F32R) for n in ("a_qh", "a_ql", "a_kh", "a_kl"))
        a_qs, a_ks = sb("a_qs", [3 * DH, H0, N], F32R), sb("a_ks", [3 * DH, H0, N], F32R)
        a_s, a_p, a_pT = (sb(n, [P, 2, 2, 256]) for n in ("a_s", "a_p", "a_pT"))
        a_max, a_sum, a_inv = (sb(n, [P, 2, NC]) for n in ("a_max", "a_sum", "a_inv"))
        a_oT = sb("a_oT", [P, 2, 256])
        x1 = sb("x1", [P, NC, D])
        a_y = a_res
        x1_h, x1_l = sb("x1_h", [P, NC, D], F32R), sb("x1_l", [P, NC, D], F32R)
        b_xT, b_res, b_t, x2 = (sb(n, [P, 2, 256]) for n in ("b_xT", "b_res", "b_t", "x2"))
        b_near_h, b_near_l = sb("b_near_h", [P, 2, 256], F32R), sb("b_near_l", [P, 2, 256], F32R)
        b_f, b_diag = sb("b_f", [P, NC, 2]), sb("b_diag", [P, NC, P])
        b_s, b_p, x3 = (sb(n, [P, 2, 256]) for n in ("b_s", "b_p", "x3"))
        b_y, b_pT, b_mix, b_y2 = b_t, b_xT, b_s, b_t
        b_nf = sb("b_nf", [P, NC, N])
        b_min, b_nm, b_sum, b_inv = (sb(n, [P, NC]) for n in ("b_min", "b_nm", "b_sum", "b_inv"))
        c_res = sb("c_res", [P, NC, D])
        c_f, c_diag = sb("c_f", [P, NC, H3, 2]), sb("c_diag", [P, NC, H3, P])
        x3_h, x3_l = sb("x3_h", [P, NC, D], F32R), sb("x3_l", [P, NC, D], F32R)
        c_s, c_p, c_e = (sb(n, [P, 2, 2, 256]) for n in ("c_s", "c_p", "c_e"))
        c_pT_h, c_pT_l, c_mix_h, c_mix_l = (sb(n, [P, 2, 2, 256], F32R) for n in
                                            ("c_pT_h", "c_pT_l", "c_mix_h", "c_mix_l"))
        c_xT = c_e[:, 0]
        c_nf = sb("c_nf", [P, 2, NC, N])
        c_min, c_nm, c_sum, c_inv = (sb(n, [P, 2, NC]) for n in ("c_min", "c_nm", "c_sum", "c_inv"))
        c_hT = sb("c_hT", [P, HC, 256])
        c_h2 = sb("c_h2", [P, NC, D + 2])
        c_diag5 = sb("c_diag5", [P, NC, P])
        c_s5, c_p5, c_pT5, c_e5, c_o5, c_out = (
            sb(n, [P, 2, 256]) for n in ("c_s5", "c_p5", "c_pT5", "c_e5", "c_o5", "c_out"))
        c_o5T, c_y, c_hid, c_res5, c_n = c_s5, c_p5, c_pT5, c_e5, c_o5
        c_nf5 = sb("c_nf5", [P, NC, N])
        c_min5, c_nm5, c_sum5, c_inv5 = (sb(n, [P, NC]) for n in ("c_min5", "c_nm5", "c_sum5", "c_inv5"))

        a3r = c_hT[:].rearrange("p k n -> p (k n)").rearrange("p (h t o) -> p h t o", h=H3, t=2)
        a2r, a5r = c_s5[:], c_p5[:]
        scratch, bor, b1r, bv_wide = c_pT5[:, 0, :], c_pT5[:, 1, :], c_e5[:, 0, :], c_o5[:, :, 0:P]
        u2_diag = [c_o5[:, :, t * P:(t + 1) * P] for t in range(2)]
        w_raw = (c_e[:, 0], c_e[:, 1], c_nf[:, 0])
        w3_raw = (c_s[:, 0], c_s[:, 1], c_p[:, 0], c_p[:, 1])
        w1j_raw = c_out[:]
        adj_i, adj_f = c_nf[:, 1].bitcast(I32), c_nf5

        class Norm:

            def __init__(self, name):
                self.stats = sb(f"{name}_stats", [P, NC, 6])
                self.mv = sb(f"{name}_mv", [P, NC, 2])
                self.ve = sb(f"{name}_ve", [P, NC])
                self.rstd = sb(f"{name}_rstd", [P, NC])
                self.in_ready = signal(f"{name}_in_ready", 1, 1)
                self.stats_ready = signal(f"{name}_stats_ready")
                self.mv_ready = signal(f"{name}_mv_ready")
                self.ve_ready = signal(f"{name}_ve_ready")
                self.rstd_ready = signal(f"{name}_rstd_ready")
                self.done = signal(f"{name}_done", 1, 1)

        n0, n1, n2, n3, n4 = (Norm(f"norm{i}") for i in range(5))

        a_loaded, b_loaded, c_loaded = signal("a_loaded"), signal("b_loaded"), signal("c_loaded")
        ident_set, consts_set = signal("ident_set"), signal("consts_set")
        adjf_set, neg_set, bvw_set = signal("adjf_set"), signal("neg_set"), signal("bvw_set")
        adjT_in, adjT_set, ab_in, ab_set = signal("adjT_in"), signal("adjT_set"), signal("ab_in"), signal("ab_set")
        u2_set, u3_set, u5_set, db_set = signal("u2_set"), signal("u3_set"), signal("u5_set"), signal("db_set")
        scr = signal("scratch_written")
        x_loaded = signal("x_loaded", step=16)
        xT_in, xT_set, xT_low_set, q_in, k_in, v_in, v_set = (
            signal(n) for n in ("xT_in", "xT_set", "xT_low_set", "q_in", "k_in", "v_in", "v_set"))
        qh_set, ql_set, kh_set, kl_set = (signal(n) for n in ("qh_set", "ql_set", "kh_set", "kl_set"))
        q_stacked, k_stacked = (signal(n, step=16 * 3 * HG) for n in ("q_stacked", "k_stacked"))
        a_res_set = signal("a_res_set")
        u2d_set, u2_in, u2_rows_set = signal("u2d_set"), signal("u2_in"), signal("u2_rows_set")
        x3_high_set, x3_low_set, w3_high_set = signal("x3_high_set"), signal("x3_low_set"), signal("w3_high_set")
        cpT_high_set, cm_high_set = signal("cpT_high_set", H3), signal("cm_high_set", H3)
        near_high_set, w1j_high_set = signal("near_high_set"), signal("w1j_high_set")
        w_high_set, w_low_set = signal("w_high_set"), signal("w_low_set")
        x1_high_set, x1_low_set = signal("x1_high_set"), signal("x1_low_set")
        s_in, p_set, inv_set = (signal(n, H0) for n in ("s_in", "p_set", "inv_set"))
        s_set = signal("s_set", H0, 1)
        pn_set, pT_in, pT_set = (signal(n, H0, 2) for n in ("pn_set", "pT_in", "pT_set"))
        o_in = signal("o_in", H0, 1)
        oT_set, ao_in = signal("oT_set"), signal("ao_in")
        bxT_in, bxT_set, near_in, b_res_set = signal("bxT_in"), signal("bxT_set"), signal("near_in", 1, 1), signal("b_res_set", 1, 1)
        near_set, yi_in, yj_in, yi_read = (signal(n) for n in ("near_set", "yi_in", "yj_in", "yi_read"))
        bf_set, bd_set = signal("bf_set"), signal("bd_set")
        bs_in, bnf_set, bs_set, bnm_set, bp_set, binv_set = (
            signal(n) for n in ("bs_in", "bnf_set", "bs_set", "bnm_set", "bp_set", "binv_set"))
        bpT_in, bpT_set, bm_in, bm_set, bo_in = (
            signal("bpT_in"), signal("bpT_set"), signal("bm_in"), signal("bm_set"), signal("bo_in"))
        cxT_in, cxT_set, cf_in, cf_set, cd_set, c_res_set = (
            signal("cxT_in"), signal("cxT_set"), signal("cf_in"), signal("cf_set"), signal("cd_set"), signal("c_res_set", 1, 1))
        cs_in, cnf_set, cnm_set, cp_set, cinv_set = (
            signal(n, H3) for n in ("cs_in", "cnf_set", "cnm_set", "cp_set", "cinv_set"))
        cs_set = signal("cs_set", H3, 2)
        cpn_set, cpT_in = signal("cpn_set", H3, 2), signal("cpT_in", H3, 2)
        cpT_set, cm_in, cm_set, ch_in, ce_set, cg_set, ch_set = (
            signal(n, H3, 1 if n in ("cm_in", "cpT_set") else 0) for n in ("cpT_set", "cm_in", "cm_set", "ch_in", "ce_set", "cg_set", "ch_set"))
        h2_in, h2a_set, h2b_set, d5_set = signal("h2_in"), signal("h2a_set"), signal("h2b_set", 1, 1), signal("d5_set")
        s5_in, nf5_set, s5_set, nm5_set, p5_set, inv5_set = (
            signal(n) for n in ("s5_in", "nf5_set", "s5_set", "nm5_set", "p5_set", "inv5_set"))
        pT5_in, pT5_set, m5_in, e5_set, g5_set, o5_set = (
            signal(n) for n in ("pT5_in", "pT5_set", "m5_in", "e5_set", "g5_set", "o5_set"))
        o5T_in, o5T_set, res5_set, hid_in, hid_set, y_in = (
            signal("o5T_in"), signal("o5T_set"), signal("res5_set"), signal("hid_in"), signal("hid_set"),
            signal("y_in"))
        ng_set = signal("ng_set")
        stored = signal("stored", 1, 1, step=16)

        block = ctx.enter_context(nc.Block())

        def run(eng, engine, steps, end=G):
            def iteration(i, whole):
                for delay, stream, what, k in ORDERS[engine]:
                    if whole or 0 <= i - delay < G:
                        steps[stream, what](i - delay, k)

            for i in range(BEHIND):
                iteration(i, False)
            with eng.Fori(BEHIND, end) as i:
                iteration(i, True)
            for i in range(end, G + BEHIND):
                iteration(i, False)

        rows = lambda w: w.rearrange("(c p) o -> p c o", p=P)
        wide = lambda v: v.partition_broadcast(P)

        def graph_rows(t, g):
            return t.rearrange("g (c p) f -> g p c f", p=P)[g]

        def grant(eng, *signals):
            for sig in signals:
                eng.sem_inc(sig.sem, sig.credit * sig.step)

        passed = {}

        def wait_apart(eng, *waits):
            for sig, value in waits:
                eng.wait_ge(sig.sem, value)
            eng.sem_inc(passed[eng], 1)

        @block.sync
        def _(sp):
            grant(sp, stored)
            loads_a = [(adj_i, rows(adj)), (w_raw[0], rows(Wq)), (bqc[:], bq),
                       (w_raw[1], rows(Wk)), (bkc[:], bk), (w_raw[2], rows(Wv)),
                       (wo[:], rows(Wo)), (bvc[:], bv), (bor, wide(bo))]
            loads_b = [(w1i[:], rows(W1i)), (w1j_raw, rows(W1j)), (b1r, wide(b1m)), (w2[:], rows(W2)),
                       (a2r[:, 0, :], wide(a2s)), (a2r[:, 1, :], wide(a2d))]
            loads_c = [(w3_raw[h], rows(W3[h])) for h in range(H3)]
            loads_c += [(a3r, wide(a3.rearrange("h (t o) -> h t o", t=2))), (w5[:, :, 0:D], rows(Wout)),
                        (a5r, wide(aout.rearrange("(t o) -> t o", t=2))), (wf1[:], rows(Wf1)), (bf1c[:], bf1),
                        (wf2[:], rows(Wf2)), (bf2r[:], wide(bf2)), (gammar[:], wide(gamma)), (betar[:], wide(beta))]
            sp.dma_start(a_x[:], graph_rows(x, 0)).then_inc(x_loaded.sem, 16)
            for sig, loads in ((a_loaded, loads_a), (b_loaded, loads_b), (c_loaded, loads_c)):
                for dst, src in loads:
                    sp.dma_start(dst, src).then_inc(sig.sem, 16)

            def load_next(g, h):
                if h or (isinstance(g, int) and g == G - 1):
                    return
                sp.wait_ge(xT_in.sem, xT_in.at(g))
                sp.wait_ge(a_res_set.sem, a_res_set.at(g))
                sp.dma_start(a_x[:], graph_rows(x, g + 1)).then_inc(x_loaded.sem, 16)

            def stack(dst, parts, low_set, stacked):
                def step(g, _):
                    sp.wait_ge(low_set.sem, low_set.at(g))
                    for r, part in enumerate(parts):
                        for j in range(HG):
                            sp.dma_start(dst[r * DH:(r + 1) * DH, j:H0:HG, :].bitcast(F32),
                                         part[j * DH:(j + 1) * DH, :, :].bitcast(F32)).then_inc(stacked.sem, 16)
                return step

            def store(g, _):
                sp.wait_ge(n4.done.sem, n4.done.at(g))
                sp.dma_start(graph_rows(out, g), c_out[:]).then_inc(stored.sem, 16)

            run(sp, SYNC, {
                ("a", "q"): stack(a_qs, (a_qh, a_ql, a_qh), ql_set, q_stacked),
                ("a", "k"): stack(a_ks, (a_kh, a_kh, a_kl), kl_set, k_stacked),
                ("a", "mix"): load_next, ("d", "norm4"): store,
            }, end=G - 1)
            sp.wait_ge(stored.sem, stored.at(G - 1))

        LOADED = {"a": 9 * 16, "b": 6 * 16, "c": (H3 + 9) * 16}

        @block.tensor
        def _(pe):
            def turn(dst, src):
                for r in range(2):
                    for c in range(2):
                        last = pe.transpose(dst[:, c, r * P:(r + 1) * P], src[:, r, c * P:(c + 1) * P], ident[:])
                return last

            def product(dst, lhsT, rhs, chunks=2):
                for m in range(2):
                    for k in range(chunks):
                        last = pe.matmul(dst[:, m, :], lhsT[:, k, m * P:(m + 1) * P], rhs[:, k, :],
                                         start=(k == 0), stop=(k == chunks - 1))
                return last

            def split_product(dst, lhs_parts, rhs_parts):
                pairs = [(a, b) for i, a in enumerate(lhs_parts) for j, b in enumerate(rhs_parts) if i + j < 2]
                for m in range(2):
                    for n, (k, (a, b)) in enumerate((k, pair) for k in range(2) for pair in pairs):
                        last = pe.matmul(dst[:, m, :], a[:, k, m * P:(m + 1) * P], b[:, k, :],
                                         start=(n == 0), stop=(n == 2 * len(pairs) - 1))
                return last

            grant(pe, o_in, near_in, cm_in, pT_in, cpT_in)
            pe.wait_ge(ident_set.sem, 1)
            pe.wait_ge(adjf_set.sem, 1)
            turn(bk_at, adj_f).then_inc(adjT_in.sem, 1)
            pe.wait_ge(bvw_set.sem, 1)
            for k in range(DC):
                last = pe.matmul(bk_as[:, 0, :], bv_wide[:, k, :], wo[:, k, :], start=(k == 0), stop=(k == DC - 1))
            last.then_inc(ab_in.sem, 1)
            pe.wait_ge(a_loaded.sem, LOADED["a"])
            pe.wait_ge(adjT_set.sem, 1)
            pe.wait_ge(ab_set.sem, 1)
            pe.wait_ge(w_low_set.sem, 3)
            pe.wait_ge(consts_set.sem, 2)

            def ax(g, _):
                pe.wait_ge(x_loaded.sem, x_loaded.at(g))
                pe.wait_ge(s_set.sem, s_set.at(g, -1))
                turn(bk_as, a_x).then_inc(xT_in.sem, 1)

            def aq(g, _):
                pe.wait_ge(xT_low_set.sem, xT_low_set.at(g))
                split_product(bk_as, (wq_h, wq_l), (a_xT_h, a_xT_l)).then_inc(q_in.sem, 1)

            def ak(g, _):
                pe.wait_ge(pT_set.sem, pT_set.at(g, -1))
                split_product(bk_at, (wk_h, wk_l), (a_xT_h, a_xT_l)).then_inc(k_in.sem, 1)

            def av(g, _):
                pe.wait_ge(ql_set.sem, ql_set.at(g))
                split_product(bk_as, (a_xT_h, a_xT_l), (wv_h, wv_l)).then_inc(v_in.sem, 1)

            def a_scores(g, h):
                if h == 0:
                    pe.wait_ge(q_stacked.sem, q_stacked.at(g))
                    pe.wait_ge(k_stacked.sem, k_stacked.at(g))
                    pe.wait_ge(v_set.sem, v_set.at(g))
                else:
                    pe.wait_ge(s_set.sem, s_set.at(g, h - 1))
                for m in range(NC):
                    last = pe.matmul(bk_as[:, m, :], a_qs[:, h, m * P:(m + 1) * P], a_ks[:, h, :],
                                     start=True, stop=True)
                last.then_inc(s_in.sem, 1)

            def a_turn(g, h):
                if h > 0:
                    pe.wait_ge(pT_set.sem, pT_set.at(g, h - 1))
                pe.wait_ge(pn_set.sem, pn_set.at(g, h))
                turn(bk_at, a_p[:, h % 2]).then_inc(pT_in.sem, 1)

            def a_mix(g, h):
                if h == 0:
                    pe.wait_ge(n0.in_ready.sem, n0.in_ready.at(g, -1))
                pe.wait_ge(pT_set.sem, pT_set.at(g, h))
                r, c = (h % HG) * DH, h // HG
                for k in range(NC):
                    last = pe.matmul(bk_ao[r:r + DH, c, :], a_v[:, k, h * DH:(h + 1) * DH], a_pT[:, h % 2, k, :],
                                     start=(k == 0), stop=(k == NC - 1))
                last.then_inc(o_in.sem, 1)

            def a_out(g, _):
                pe.wait_ge(oT_set.sem, oT_set.at(g))
                product(bk_ao, a_oT, wo).then_inc(ao_in.sem, 1)

            def bx(g, _):
                pe.wait_ge(n0.done.sem, n0.done.at(g))
                pe.wait_ge(n2.in_ready.sem, n2.in_ready.at(g, -1))
                turn(bk_b, x1).then_inc(bxT_in.sem, 1)

            def b_near_(g, _):
                pe.wait_ge(bxT_set.sem, bxT_set.at(g))
                pe.wait_ge(x1_low_set.sem, x1_low_set.at(g))
                split_product(bk_b, (x1_h, x1_l), (adjT,)).then_inc(near_in.sem, 1)

            def b_yi(g, _):
                pe.wait_ge(near_set.sem, near_set.at(g))
                product(bk_b, b_xT, w1i).then_inc(yi_in.sem, 1)

            def b_yj(g, _):
                pe.wait_ge(yi_read.sem, yi_read.at(g))
                split_product(bk_b, (b_near_h, b_near_l), (w1j_h, w1j_l)).then_inc(yj_in.sem, 1)

            def spread(dst, diag):
                for k in range(NC):
                    last = pe.matmul(dst[:, k * P:(k + 1) * P], ones[:], diag[:, k, :], start=True, stop=True)
                return last

            def u2_spread():
                pe.wait_ge(u2d_set.sem, 1)
                for t in range(2):
                    last = spread(bk_d[:, t, :], u2_diag[t])
                last.then_inc(u2_in.sem, 1)

            def b_scores(g, _):
                pe.wait_ge(bd_set.sem, bd_set.at(g))
                spread(bk_b[:, 0, :], b_diag).then_inc(bs_in.sem, 1)

            def b_turn(g, _):
                pe.wait_ge(bp_set.sem, bp_set.at(g))
                turn(bk_b, b_p).then_inc(bpT_in.sem, 1)

            def b_mix_(g, _):
                pe.wait_ge(bpT_set.sem, bpT_set.at(g))
                product(bk_b, x2, b_pT).then_inc(bm_in.sem, 1)

            def b_out(g, _):
                pe.wait_ge(bm_set.sem, bm_set.at(g))
                product(bk_b, b_mix, w2).then_inc(bo_in.sem, 1)

            def cx(g, _):
                pe.wait_ge(n2.done.sem, n2.done.at(g))
                pe.wait_ge(cs_set.sem, cs_set.at(g, -1))
                turn(bk_cs, x3).then_inc(cxT_in.sem, 1)

            def cf(g, _):
                pe.wait_ge(cxT_set.sem, cxT_set.at(g))
                pe.wait_ge(cpT_set.sem, cpT_set.at(g, -1))
                w = 2 * H3
                for m in range(NC):
                    for k in range(DC):
                        last = pe.matmul(bk_ct[:, 0, w * m:w * m + w], c_xT[:, k, m * P:(m + 1) * P],
                                         u3[:, k, :, :].rearrange("p h t -> p (h t)"),
                                         start=(k == 0), stop=(k == DC - 1))
                last.then_inc(cf_in.sem, 1)

            def c_scores(g, h):
                if h == 0:
                    pe.wait_ge(cd_set.sem, cd_set.at(g))
                else:
                    pe.wait_ge(cs_set.sem, cs_set.at(g, h - 1))
                spread(bk_cs[:, 0, :], c_diag[:, :, h, :]).then_inc(cs_in.sem, 1)

            def c_turn(g, h):
                if h > 0:
                    pe.wait_ge(cpT_set.sem, cpT_set.at(g, h - 1))
                pe.wait_ge(cpn_set.sem, cpn_set.at(g, h))
                turn(bk_ct, c_p[:, h % 2]).then_inc(cpT_in.sem, 1)

            def c_mix_(g, h):
                if h == 0:
                    pe.wait_ge(h2b_set.sem, h2b_set.at(g, -1))
                else:
                    pe.wait_ge(ch_set.sem, ch_set.at(g, h - 1))
                pe.wait_ge(cpT_set.sem, cpT_set.at(g, h))
                if h == 0:
                    pe.wait_ge(x3_low_set.sem, x3_low_set.at(g))
                split_product(bk_cm, (x3_h, x3_l), (c_pT_h[:, h % 2], c_pT_l[:, h % 2])).then_inc(cm_in.sem, 1)

            def c_head(g, h):
                pe.wait_ge(cm_set.sem, cm_set.at(g, h))
                split_product(bk_cm, (w3_h[:, :, h, :], w3_l[:, :, h, :]), (c_mix_h[:, h % 2], c_mix_l[:, h % 2])).then_inc(ch_in.sem, 1)

            def c_join(g, _):
                pe.wait_ge(ch_set.sem, ch_set.at(g))
                pe.wait_ge(n3.in_ready.sem, n3.in_ready.at(g, -1))
                for m, dst in enumerate((bk_d, bk_cm)):
                    flat = dst[:, :, :].rearrange("p a b -> p (a b)")[:, 0:D + 2]
                    for k in range(HC):
                        last = pe.matmul(flat, c_hT[:, k, m * P:(m + 1) * P], w5[:, k, :],
                                         start=(k == 0), stop=(k == HC - 1))
                last.then_inc(h2_in.sem, 1)

            def d_scores(g, _):
                pe.wait_ge(d5_set.sem, d5_set.at(g))
                spread(bk_d[:, 0, :], c_diag5).then_inc(s5_in.sem, 1)

            def d_turn(g, _):
                pe.wait_ge(p5_set.sem, p5_set.at(g))
                pe.wait_ge(h2b_set.sem, h2b_set.at(g))
                turn(bk_d, c_p5).then_inc(pT5_in.sem, 1)

            def d_mix(g, _):
                pe.wait_ge(pT5_set.sem, pT5_set.at(g))
                product(bk_d, c_pT5, c_h2[:, :, 0:D]).then_inc(m5_in.sem, 1)

            def d_x(g, _):
                pe.wait_ge(o5_set.sem, o5_set.at(g))
                turn(bk_d, c_o5).then_inc(o5T_in.sem, 1)

            def d_ffn1(g, _):
                pe.wait_ge(o5T_set.sem, o5T_set.at(g))
                product(bk_d, wf1, c_o5T).then_inc(hid_in.sem, 1)

            def d_ffn2(g, _):
                pe.wait_ge(hid_set.sem, hid_set.at(g))
                product(bk_d, c_hid, wf2).then_inc(y_in.sem, 1)

            def once(fn, *waits):
                def step(g, k):
                    if isinstance(g, int) and g == 0 and k == 0:
                        for sig, value in waits:
                            pe.wait_ge(sig.sem, value)
                    fn(g, k)
                return step

            def bx_first(g, k):
                bx(g, k)
                if isinstance(g, int) and g == 0:
                    u2_spread()

            run(pe, PE, {
                ("a", "x"): ax, ("a", "q"): aq, ("a", "k"): ak, ("a", "v"): av, ("a", "scores"): a_scores,
                ("a", "turn"): a_turn, ("a", "mix"): a_mix, ("a", "out"): a_out,
                ("b", "x"): once(bx_first, (b_loaded, LOADED["b"]), (u2_set, 1)), ("b", "near"): b_near_, ("b", "yi"): b_yi, ("b", "yj"): b_yj,
                ("b", "scores"): b_scores, ("b", "turn"): b_turn, ("b", "mix"): b_mix_,
                ("b", "out"): b_out,
                ("c", "x"): once(cx, (c_loaded, LOADED["c"]), (u3_set, 1), (u5_set, 1)), ("c", "f"): cf,
                ("c", "scores"): c_scores, ("c", "turn"): c_turn, ("c", "mix"): c_mix_, ("c", "head"): c_head,
                ("c", "join"): c_join, ("d", "scores"): d_scores, ("d", "turn"): d_turn, ("d", "mix"): d_mix,
                ("d", "x"): d_x, ("d", "ffn1"): d_ffn1, ("d", "ffn2"): d_ffn2,
            })

        @block.scalar
        def _(act):
            grant(act, pT_set, h2b_set)
            act.wait_ge(adjT_in.sem, 1)
            act.activation(adjT[:], bk_at[:], ACT.Copy).then_inc(adjT_set.sem, 1)
            act.wait_ge(a_loaded.sem, LOADED["a"])
            act.wait_ge(ident_set.sem, 1)
            for w_h, w in zip((wq_h, wk_h, wv_h), w_raw):
                act.activation(w_h[:], w, ACT.Copy).then_inc(w_high_set.sem, 1)

            def w1j_high():
                act.wait_ge(b_loaded.sem, LOADED["b"])
                act.activation(w1j_h[:], w1j_raw, ACT.Copy).then_inc(w1j_high_set.sem, 1)

            def copy(dst, src, filled, value, done):
                act.wait_ge(filled.sem, value)
                act.activation(dst, src, ACT.Copy).then_inc(done.sem, 1)

            def ax(g, _):
                copy(a_xT_h[:], bk_as[:], xT_in, xT_in.at(g), xT_set)

            def high(dst, bank, bias, filled, g, done):
                act.wait_ge(filled.sem, filled.at(g))
                for c in range(DC):
                    last = act.activation(dst[:, c, :], bank[:, c, :], ACT.Identity, bias=bias[:, c:c + 1])
                last.then_inc(done.sem, 1)

            def aq(g, _):
                high(a_qh, bk_as, bqc, q_in, g, qh_set)

            def ak(g, _):
                high(a_kh, bk_at, bkc, k_in, g, kh_set)

            def av(g, _):
                act.wait_ge(o_in.sem, o_in.at(g, -1))
                copy(a_v[:], bk_as[:], v_in, v_in.at(g), v_set)

            def a_scores(g, h):
                act.wait_ge(s_set.sem, s_set.at(g, h))
                act.wait_ge(pT_in.sem, pT_in.at(g, h - 2))
                for m in range(NC):
                    last = act.activation(a_p[:, h % 2, m, :], a_s[:, h % 2, m, :], ACT.Exp,
                                          bias=a_max[:, h % 2, m:m + 1], scale=-1.0, accum_out=a_sum[:, h % 2, m:m + 1])
                last.then_inc(p_set.sem, 1)

            def a_turn(g, h):
                copy(a_pT[:, h % 2], bk_at[:], pT_in, pT_in.at(g, h), pT_set)

            def a_out(g, _):
                copy(a_oT[:], bk_ao[:], o_in, o_in.at(g), oT_set)

            def gat_probs(s, p, nm, total, done):
                for m in range(NC):
                    last = act.activation(p[:, m, :], s[:, m, :], ACT.Exp, bias=nm[:, m:m + 1], scale=-1.0,
                                          accum_out=total[:, m:m + 1])
                last.then_inc(done.sem, 1)

            def bx(g, _):
                copy(x1_h[:], x1[:], n0.done, n0.done.at(g), x1_high_set)
                copy(b_xT[:], bk_b[:], bxT_in, bxT_in.at(g), bxT_set)

            def b_near_(g, _):
                copy(b_near_h[:], bk_b[:], near_in, near_in.at(g), near_high_set)

            def u2_copy():
                copy(u2_rows[:], bk_d[:], u2_in, 1, u2_rows_set)

            def diagonals(dst, col_of, done):
                for m in range(NC):
                    last = act.activation(dst[:, m, :], ident[:], ACT.Copy, scale=col_of(m))
                last.then_inc(done.sem, 1)

            def bf(g, _):
                act.wait_ge(bf_set.sem, bf_set.at(g))
                diagonals(b_diag, lambda m: b_f[:, m, 1:2], bd_set)

            def b_scores(g, _):
                act.wait_ge(bnm_set.sem, bnm_set.at(g))
                gat_probs(b_s, b_p, b_nm, b_sum, bp_set)

            def b_turn(g, _):
                copy(b_pT[:], bk_b[:], bpT_in, bpT_in.at(g), bpT_set)

            def b_mix_(g, _):
                copy(b_mix[:], bk_b[:], bm_in, bm_in.at(g), bm_set)

            def cx(g, _):
                copy(x3_h[:], x3[:], n2.done, n2.done.at(g), x3_high_set)
                copy(c_xT[:], bk_cs[:], cxT_in, cxT_in.at(g), cxT_set)

            def cf(g, _):
                act.wait_ge(cf_set.sem, cf_set.at(g))
                for h in range(H3):
                    for m in range(NC):
                        last = act.activation(c_diag[:, m, h, :], ident[:], ACT.Copy, scale=c_f[:, m, h, 1:2])
                last.then_inc(cd_set.sem, 1)

            def c_scores(g, h):
                act.wait_ge(cnm_set.sem, cnm_set.at(g, h))
                act.wait_ge(cpT_in.sem, cpT_in.at(g, h - 2))
                i = h % 2
                gat_probs(c_s[:, i], c_p[:, i], c_nm[:, i], c_sum[:, i], cp_set)

            def c_turn(g, h):
                copy(c_pT_h[:, h % 2], bk_ct[:], cpT_in, cpT_in.at(g, h), cpT_high_set)

            def c_mix_(g, h):
                copy(c_mix_h[:, h % 2], bk_cm[:], cm_in, cm_in.at(g, h), cm_high_set)

            def w3_high():
                act.wait_ge(c_loaded.sem, LOADED["c"])
                for h in range(H3):
                    last = act.activation(w3_h[:, :, h, :], w3_raw[h], ACT.Copy)
                last.then_inc(w3_high_set.sem, 1)

            def c_head(g, h):
                act.wait_ge(ch_in.sem, ch_in.at(g, h))
                act.activation(c_e[:, h % 2], bk_cm[:], ACT.Exp).then_inc(ce_set.sem, 1)

            def c_join(g, _):
                act.wait_ge(h2_in.sem, h2_in.at(g))
                act.activation(c_h2[:, 1, :], bk_cm[:, :, :].rearrange("p a b -> p (a b)")[:, 0:D + 2],
                               ACT.Copy).then_inc(h2b_set.sem, 1)
                act.wait_ge(h2a_set.sem, h2a_set.at(g))
                act.wait_ge(h2b_set.sem, h2b_set.at(g))
                diagonals(c_diag5, lambda m: c_h2[:, m, D + 1:D + 2], d5_set)

            def d_scores(g, _):
                act.wait_ge(nm5_set.sem, nm5_set.at(g))
                gat_probs(c_s5, c_p5, c_nm5, c_sum5, p5_set)

            def d_turn(g, _):
                copy(c_pT5[:], bk_d[:], pT5_in, pT5_in.at(g), pT5_set)

            def d_mix(g, _):
                act.wait_ge(m5_in.sem, m5_in.at(g))
                act.wait_ge(inv5_set.sem, inv5_set.at(g))
                for m in range(NC):
                    last = act.activation(c_e5[:, m, :], bk_d[:, m, :], ACT.Exp, scale=c_inv5[:, m:m + 1])
                last.then_inc(e5_set.sem, 1)

            def d_x(g, _):
                copy(c_o5T[:], bk_d[:], o5T_in, o5T_in.at(g), o5T_set)

            def d_ffn1(g, _):
                act.wait_ge(hid_in.sem, hid_in.at(g))
                for c in range(DC):
                    last = act.activation(c_hid[:, c, :], bk_d[:, c, :], ACT.Relu, bias=bf1c[:, c:c + 1])
                last.then_inc(hid_set.sem, 1)

            def after(fn, *setups):
                def step(g, k):
                    fn(g, k)
                    if isinstance(g, int) and g == 0:
                        for setup in setups:
                            setup()
                return step

            run(act, SCALAR, {
                ("a", "x"): ax, ("a", "q"): aq, ("a", "k"): ak, ("a", "v"): after(av, w1j_high, w3_high),
                ("a", "scores"): a_scores, ("a", "turn"): a_turn, ("a", "out"): a_out,
                ("b", "x"): after(bx, u2_copy), ("b", "near"): b_near_, ("b", "f"): bf, ("b", "scores"): b_scores, ("b", "turn"): b_turn,
                ("b", "mix"): b_mix_,
                ("c", "x"): cx, ("c", "f"): cf, ("c", "scores"): c_scores, ("c", "turn"): c_turn, ("c", "mix"): c_mix_,
                ("c", "head"): c_head, ("c", "join"): c_join,
                ("d", "scores"): d_scores, ("d", "turn"): d_turn, ("d", "mix"): d_mix, ("d", "x"): d_x,
                ("d", "ffn1"): d_ffn1,
            })

        @block.vector
        def _(dve):
            passed[dve] = ctx.enter_context(nc.semaphore("vector_waits_passed"))
            grant(dve, n0.in_ready, n1.in_ready, n2.in_ready, n3.in_ready, n4.in_ready, s_set, cs_set, cpT_set,
                  n0.done, n1.done, n2.done, n3.done, n4.done)
            dve.wait_ge(a_loaded.sem, LOADED["a"])
            dve.tensor_copy(adj_f[:], adj_i).then_inc(adjf_set.sem, 1)
            dve.wait_ge(adjf_set.sem, 1)
            dve.tensor_scalar(neg[:], adj_f[:], 0.0, MASKED, ALU.is_equal, ALU.mult).then_inc(neg_set.sem, 1)
            dve.tensor_reduce(deg[:], adj_f[:], AX_X, ALU.add).then_inc(neg_set.sem, 1)
            dve.wait_ge(consts_set.sem, 2)
            for k in range(DC):
                last = dve.tensor_scalar(bv_wide[:, k, :], ones[:], bvc[:, k:k + 1], None, ALU.mult)
            last.then_inc(bvw_set.sem, 1)
            dve.wait_ge(ab_in.sem, 1)
            dve.tensor_tensor(attn_bias[:], bk_as[:, 0, :], bor, ALU.add).then_inc(ab_set.sem, 1)
            for n, (w_h, w_l) in enumerate(((wq_h, wq_l), (wk_h, wk_l), (wv_h, wv_l))):
                dve.wait_ge(w_high_set.sem, n + 1)
                dve.tensor_tensor(w_l[:], w_raw[n], w_h[:].bitcast(F32), ALU.subtract)\
                    .then_inc(w_low_set.sem, 1)
            dve.wait_ge(neg_set.sem, 2)
            dve.wait_ge(ident_set.sem, 1)

            written = [0]

            def fold(dst, w, a):
                if written[0]:
                    dve.wait_ge(scr.sem, written[0])
                written[0] += 1
                return dve.tensor_tensor_reduce(scratch, w, a, 1.0, 0.0, ALU.mult, ALU.add, dst)

            def fold_b():
                dve.wait_ge(b_loaded.sem, LOADED["b"])
                for k in range(DC):
                    for t in range(2):
                        fold(u2[:, k, t:t + 1], w2[:, k, :], a2r[:, t, :]).then_inc(scr.sem, 1)
                for m in range(NC):
                    last = dve.tensor_scalar(deg_bias[:, m, :], b1r, deg[:, m:m + 1], None, ALU.mult)
                last.then_inc(db_set.sem, 1)
                dve.wait_ge(w1j_high_set.sem, 1)
                dve.tensor_tensor(w1j_l[:], w1j_raw, w1j_h[:].bitcast(F32), ALU.subtract).then_inc(scr.sem, 1)
                written[0] += 1
                dve.wait_ge(scr.sem, written[0])
                for t in range(2):
                    for k in range(DC):
                        last = dve.tensor_scalar(u2_diag[t][:, k, :], ident[:], u2[:, k, t:t + 1], None, ALU.mult)
                last.then_inc(u2d_set.sem, 1)
                dve.sem_inc(u2_set.sem, 1)

            def fold_c():
                dve.wait_ge(c_loaded.sem, LOADED["c"])
                for k in range(DC):
                    for h in range(H3):
                        for t in range(2):
                            fold(u3[:, k, h, t:t + 1], w3_raw[h][:, k, :], a3r[:, h, t, :]).then_inc(scr.sem, 1)
                for k in range(HC):
                    for t in range(2):
                        fold(w5[:, k, D + t:D + t + 1], w5[:, k, 0:D], a5r[:, t, :]).then_inc(scr.sem, 1)
                dve.wait_ge(w3_high_set.sem, 1)
                written[0] += H3
                for h in range(H3):
                    dve.tensor_tensor(w3_l[:, :, h, :], w3_raw[h], w3_h[:, :, h, :].bitcast(F32), ALU.subtract)\
                        .then_inc(scr.sem, 1)
                dve.wait_ge(scr.sem, written[0])
                dve.sem_inc(u3_set.sem, 1)
                dve.sem_inc(u5_set.sem, 1)

            def norm_stats(n, g, src):
                dve.wait_ge(n.in_ready.sem, n.in_ready.at(g))
                for m in range(NC):
                    last = dve.bn_stats(n.stats[:, m, :], src[:, m, :])
                last.then_inc(n.stats_ready.sem, 1)
                wait_apart(dve, (n.stats_ready, n.stats_ready.at(g)))
                for m in range(NC):
                    last = dve.bn_aggr(n.mv[:, m, :], n.stats[:, m, :])
                last.then_inc(n.mv_ready.sem, 1)
                dve.wait_ge(n.mv_ready.sem, n.mv_ready.at(g))
                dve.tensor_scalar(n.ve[:], n.mv[:, :, 1], EPS, None, ALU.add).then_inc(n.ve_ready.sem, 1)

            def norm_apply(n, g, src, dst, *free):
                dve.wait_ge(n.rstd_ready.sem, n.rstd_ready.at(g))
                for sig, value in free:
                    dve.wait_ge(sig.sem, value)
                for m in range(NC):
                    last = dve.tensor_scalar(dst[:, m, :], src[:, m, :], n.mv[:, m, 0:1], n.rstd[:, m:m + 1],
                                             ALU.subtract, ALU.mult)
                last.then_inc(n.done.sem, 1)

            def low(dst, bank, bias, high, high_set, g, done):
                dve.wait_ge(high_set.sem, high_set.at(g))
                for c in range(DC):
                    last = dve.scalar_tensor_tensor(dst[:, c, :], bank[:, c, :], bias[:, c:c + 1],
                                                    high[:, c, :].bitcast(F32), ALU.add, ALU.subtract)
                last.then_inc(done.sem, 1)

            def ax(g, _):
                dve.wait_ge(xT_set.sem, xT_set.at(g))
                dve.tensor_tensor(a_xT_l[:], bk_as[:], a_xT_h[:].bitcast(F32), ALU.subtract).then_inc(xT_low_set.sem, 1)

            def aq(g, _):
                low(a_ql, bk_as, bqc, a_qh, qh_set, g, ql_set)

            def ak(g, _):
                low(a_kl, bk_at, bkc, a_kh, kh_set, g, kl_set)

            def a_scores(g, h):
                wait_apart(dve, (s_in, s_in.at(g, h)))
                for m in range(NC):
                    last = dve.tensor_tensor_reduce(a_s[:, h % 2, m, :], bk_as[:, m, :], neg[:, m, :], -SCALE, HUGE,
                                                    ALU.add, ALU.min, a_max[:, h % 2, m:m + 1])
                last.then_inc(s_set.sem, 1)

            def a_normalise(g, h):
                dve.wait_ge(p_set.sem, p_set.at(g, h))
                dve.reciprocal(a_inv[:, h % 2], a_sum[:, h % 2]).then_inc(inv_set.sem, 1)

            def a_out(g, _):
                dve.wait_ge(ao_in.sem, ao_in.at(g))
                dve.wait_ge(a_res_set.sem, a_res_set.at(g))
                dve.tensor_tensor(a_y[:], bk_ao[:], a_res[:], ALU.add).then_inc(n0.in_ready.sem, 1)
                norm_stats(n0, g, a_y)

            def a_norm(g, _):
                norm_apply(n0, g, a_y, x1, (near_in, near_in.at(g, -1)), (b_res_set, b_res_set.at(g, -1)))

            def b_near_(g, _):
                dve.wait_ge(near_high_set.sem, near_high_set.at(g))
                dve.tensor_tensor(b_near_l[:], bk_b[:], b_near_h[:].bitcast(F32), ALU.subtract).then_inc(near_set.sem, 1)

            def b_yi(g, _):
                dve.wait_ge(yi_in.sem, yi_in.at(g))
                dve.wait_ge(b_res_set.sem, b_res_set.at(g))
                for m in range(NC):
                    last = dve.scalar_tensor_tensor(b_t[:, m, :], bk_b[:, m, :], deg[:, m:m + 1], b_res[:, m, :],
                                                    ALU.mult, ALU.add)
                last.then_inc(yi_read.sem, 1)

            def b_yj(g, _):
                dve.wait_ge(yi_read.sem, yi_read.at(g))
                dve.wait_ge(yj_in.sem, yj_in.at(g))
                dve.tensor_tensor(b_y[:], bk_b[:], b_t[:], ALU.add).then_inc(n1.in_ready.sem, 1)
                norm_stats(n1, g, b_y)

            def b_norm1(g, _):
                norm_apply(n1, g, b_y, x2)

            def bf(g, _):
                if isinstance(g, int) and g == 0:
                    dve.wait_ge(u2_rows_set.sem, 1)
                wait_apart(dve, (n1.done, n1.done.at(g)))
                for t, products in enumerate((b_t, b_s)):
                    for m in range(NC):
                        last = dve.tensor_tensor_reduce(products[:, m, :], x2[:, m, :], u2_rows[:, t, :], 1.0, 0.0,
                                                        ALU.mult, ALU.add, b_f[:, m, t:t + 1])
                last.then_inc(bf_set.sem, 1)

            def gat_scores(filled, masked, src, nf, s, low, nm, slope, s_done, s_at, nm_done):
                wait_apart(dve, masked, filled)
                for m in range(NC):
                    last = dve.tensor_tensor_reduce(s[:, m, :], src, nf[:, m, :], -1.0, HUGE, ALU.add, ALU.min,
                                                    low[:, m:m + 1])
                last.then_inc(s_done.sem, 1)
                dve.wait_ge(s_done.sem, s_at)
                dve.scalar_tensor_tensor(nm[:], low[:], slope, low[:], ALU.mult, ALU.min)
                dve.scalar_tensor_tensor(s[:], s[:], slope, s[:], ALU.mult, ALU.min).then_inc(nm_done.sem, 1)

            def b_scores(g, _):
                gat_scores((bs_in, bs_in.at(g)), (bnf_set, bnf_set.at(g)), bk_b[:, 0, :], b_nf, b_s, b_min, b_nm,
                           SLOPE2, bs_set, bs_set.at(g), bnm_set)

            def b_turn(g, _):
                dve.wait_ge(bp_set.sem, bp_set.at(g))
                dve.reciprocal(b_inv[:], b_sum[:]).then_inc(binv_set.sem, 1)

            def b_out(g, _):
                dve.wait_ge(bo_in.sem, bo_in.at(g))
                dve.wait_ge(binv_set.sem, binv_set.at(g))
                for m in range(NC):
                    last = dve.scalar_tensor_tensor(b_y2[:, m, :], bk_b[:, m, :], b_inv[:, m:m + 1], x2[:, m, :],
                                                    ALU.mult, ALU.add)
                last.then_inc(n2.in_ready.sem, 1)
                norm_stats(n2, g, b_y2)

            def b_norm2(g, _):
                norm_apply(n2, g, b_y2, x3, (cm_in, cm_in.at(g, -1)), (c_res_set, c_res_set.at(g, -1)))

            def cf(g, _):
                dve.wait_ge(cf_in.sem, cf_in.at(g))
                dve.tensor_copy(c_f[:].rearrange("p m h t -> p (m h t)"), bk_ct[:, 0, 0:2 * NC * H3]).then_inc(cf_set.sem, 1)

            def c_scores(g, h):
                i = h % 2
                gat_scores((cs_in, cs_in.at(g, h)), (cnf_set, cnf_set.at(g, h)), bk_cs[:, 0, :], c_nf[:, i], c_s[:, i],
                           c_min[:, i], c_nm[:, i], SLOPE3, cs_set, cs_set.at(g, h), cnm_set)

            def c_normalise(g, h):
                dve.wait_ge(cp_set.sem, cp_set.at(g, h))
                dve.reciprocal(c_inv[:, h % 2], c_sum[:, h % 2]).then_inc(cinv_set.sem, 1)

            def c_turn(g, h):
                dve.wait_ge(cpT_high_set.sem, cpT_high_set.at(g, h))
                dve.tensor_tensor(c_pT_l[:, h % 2], bk_ct[:], c_pT_h[:, h % 2].bitcast(F32), ALU.subtract)\
                    .then_inc(cpT_set.sem, 1)

            def c_mix_(g, h):
                dve.wait_ge(cm_high_set.sem, cm_high_set.at(g, h))
                dve.tensor_tensor(c_mix_l[:, h % 2], bk_cm[:], c_mix_h[:, h % 2].bitcast(F32), ALU.subtract)\
                    .then_inc(cm_set.sem, 1)

            def c_head(g, h):
                dve.wait_ge(ce_set.sem, ce_set.at(g, h))
                dve.tensor_scalar(c_e[:, h % 2], c_e[:, h % 2], 1.0, -1.0, ALU.min, ALU.add).then_inc(cg_set.sem, 1)
                dve.wait_ge(cg_set.sem, cg_set.at(g, h))
                dve.tensor_tensor(c_hT[:, h * DC:(h + 1) * DC, :], bk_cm[:], c_e[:, h % 2], ALU.max).then_inc(ch_set.sem, 1)

            def c_join(g, _):
                dve.wait_ge(h2_in.sem, h2_in.at(g))
                dve.tensor_copy(c_h2[:, 0, :], bk_d[:, :, :].rearrange("p a b -> p (a b)")[:, 0:D + 2]).then_inc(h2a_set.sem, 1)

            def d_scores(g, _):
                gat_scores((s5_in, s5_in.at(g)), (nf5_set, nf5_set.at(g)), bk_d[:, 0, :], c_nf5, c_s5, c_min5, c_nm5,
                           SLOPE3, s5_set, s5_set.at(g), nm5_set)

            def d_turn(g, _):
                dve.wait_ge(p5_set.sem, p5_set.at(g))
                dve.reciprocal(c_inv5[:], c_sum5[:]).then_inc(inv5_set.sem, 1)

            def d_mix(g, _):
                dve.wait_ge(e5_set.sem, e5_set.at(g))
                dve.tensor_scalar(c_e5[:], c_e5[:], 1.0, -1.0, ALU.min, ALU.add).then_inc(g5_set.sem, 1)
                dve.wait_ge(g5_set.sem, g5_set.at(g))
                for m in range(NC):
                    last = dve.scalar_tensor_tensor(c_o5[:, m, :], bk_d[:, m, :], c_inv5[:, m:m + 1], c_e5[:, m, :],
                                                    ALU.mult, ALU.max)
                last.then_inc(o5_set.sem, 1)

            def d_ffn2(g, _):
                dve.wait_ge(y_in.sem, y_in.at(g))
                dve.wait_ge(res5_set.sem, res5_set.at(g))
                dve.tensor_tensor(c_y[:], bk_d[:], c_res5[:], ALU.add).then_inc(n3.in_ready.sem, 1)
                norm_stats(n3, g, c_y)

            def d_norm3(g, _):
                norm_apply(n3, g, c_y, c_n)
                dve.wait_ge(n3.done.sem, n3.done.at(g))
                dve.tensor_tensor(c_n[:], c_n[:], gammar[:].unsqueeze(1).to_broadcast([P, NC, D]), ALU.mult)\
                    .then_inc(ng_set.sem, 1)
                dve.wait_ge(ng_set.sem, ng_set.at(g))
                dve.wait_ge(c_res_set.sem, c_res_set.at(g))
                dve.tensor_tensor(c_n[:], c_n[:], c_res[:], ALU.add).then_inc(n4.in_ready.sem, 1)
                norm_stats(n4, g, c_n)

            def d_norm4(g, _):
                norm_apply(n4, g, c_n, c_out, (stored, stored.at(g, -1)))

            def after(fn, *setups):
                def step(g, k):
                    fn(g, k)
                    if isinstance(g, int) and g == 0:
                        for setup in setups:
                            setup()
                return step

            run(dve, DVE, {
                ("a", "x"): ax,
                ("a", "q"): aq, ("a", "k"): after(ak, fold_b, fold_c), ("a", "scores"): a_scores, ("a", "normalise"): a_normalise,
                ("a", "out"): a_out, ("a", "norm"): a_norm,
                ("b", "near"): b_near_, ("b", "yi"): b_yi, ("b", "yj"): b_yj, ("b", "f"): bf, ("b", "scores"): b_scores,
                ("b", "turn"): b_turn, ("b", "out"): b_out, ("b", "norm1"): b_norm1, ("b", "norm2"): b_norm2,
                ("c", "f"): cf, ("c", "scores"): c_scores, ("c", "normalise"): c_normalise, ("c", "turn"): c_turn, ("c", "mix"): c_mix_,
                ("c", "head"): c_head, ("c", "join"): c_join, ("d", "scores"): d_scores, ("d", "turn"): d_turn,
                ("d", "mix"): d_mix, ("d", "ffn2"): d_ffn2, ("d", "norm3"): d_norm3, ("d", "norm4"): d_norm4,
            })

        @block.gpsimd
        def _(pool):
            passed[pool] = ctx.enter_context(nc.semaphore("pool_waits_passed"))
            grant(pool, pn_set, cpn_set, b_res_set, c_res_set)
            pool.memset(ident[:], 0.0).then_inc(consts_set.sem, 1)
            pool.memset(ones[:], 1.0).then_inc(consts_set.sem, 1)
            pool.memset(minus_half[:], -0.5).then_inc(consts_set.sem, 1)
            pool.wait_ge(consts_set.sem, 3)
            pool.affine_select(out=ident[:], in_=ident[:], compare_op=ALU.not_equal, fill=1.0, base=0,
                               pattern=[[-1, P]], channel_multiplier=1).then_inc(ident_set.sem, 1)

            def power(n):
                def step(g, _):
                    pool.wait_ge(n.ve_ready.sem, n.ve_ready.at(g))
                    pool.tensor_tensor(n.rstd[:], n.ve[:], minus_half[:], ALU.pow).then_inc(n.rstd_ready.sem, 1)
                return step

            pool.wait_ge(ab_set.sem, 1)

            def a_mix(g, h):
                if h:
                    return
                pool.wait_ge(x_loaded.sem, x_loaded.at(g))
                pool.wait_ge(n0.done.sem, n0.done.at(g, -1))
                pool.tensor_tensor(a_res[:], a_x[:], attn_bias[:].unsqueeze(1).to_broadcast([P, NC, D]), ALU.add)\
                    .then_inc(a_res_set.sem, 1)

            def divide(p, inv, done):
                for m in range(NC):
                    last = pool.tensor_scalar(p[:, m, :], p[:, m, :], inv[:, m:m + 1], 1.0, ALU.mult, ALU.mult)
                last.then_inc(done.sem, 1)

            def a_normalise(g, h):
                wait_apart(pool, (inv_set, inv_set.at(g, h)))
                divide(a_p[:, h % 2], a_inv[:, h % 2], pn_set)

            def add_mask(nf, f1, done):
                for m in range(NC):
                    last = pool.tensor_scalar(nf[:, m, :], neg[:, m, :], f1(m), 1.0, ALU.add, ALU.mult)
                last.then_inc(done.sem, 1)

            def bf(g, _):
                wait_apart(pool, (bf_set, bf_set.at(g)))
                add_mask(b_nf, lambda m: b_f[:, m, 0:1], bnf_set)

            def c_mask(g, h):
                wait_apart(pool, (cf_set, cf_set.at(g)), (cs_set, cs_set.at(g, h - 2)))
                add_mask(c_nf[:, h % 2], lambda m: c_f[:, m, h, 0:1], cnf_set)

            def cf(g, _):
                c_mask(g, 0)
                c_mask(g, 1)

            def c_join(g, _):
                c_residual(g)
                wait_apart(pool, (h2a_set, h2a_set.at(g)), (h2b_set, h2b_set.at(g)))
                add_mask(c_nf5, lambda m: c_h2[:, m, D:D + 1], nf5_set)

            def bx(g, _):
                pool.wait_ge(x1_high_set.sem, x1_high_set.at(g))
                pool.tensor_tensor(x1_l[:], x1[:], x1_h[:].bitcast(F32), ALU.subtract).then_inc(x1_low_set.sem, 1)
                pool.tensor_tensor(b_res[:], x1[:], deg_bias[:], ALU.add).then_inc(b_res_set.sem, 1)

            def cx(g, _):
                pool.wait_ge(x3_high_set.sem, x3_high_set.at(g))
                pool.tensor_tensor(x3_l[:], x3[:], x3_h[:].bitcast(F32), ALU.subtract).then_inc(x3_low_set.sem, 1)

            def c_residual(g):
                pool.wait_ge(n2.done.sem, n2.done.at(g))
                pool.wait_ge(n4.in_ready.sem, n4.in_ready.at(g, -1))
                pool.tensor_tensor(c_res[:], x3[:], betar[:].unsqueeze(1).to_broadcast([P, NC, D]), ALU.add)\
                    .then_inc(c_res_set.sem, 1)

            def c_normalise(g, h):
                wait_apart(pool, (cinv_set, cinv_set.at(g, h)))
                divide(c_p[:, h % 2], c_inv[:, h % 2], cpn_set)
                if h + 2 < H3:
                    c_mask(g, h + 2)

            def d_x(g, _):
                pool.wait_ge(o5_set.sem, o5_set.at(g))
                pool.tensor_tensor(c_res5[:], c_o5[:], bf2r[:].unsqueeze(1).to_broadcast([P, NC, D]), ALU.add)\
                    .then_inc(res5_set.sem, 1)

            def once(fn, sig, value):
                def step(g, k):
                    if isinstance(g, int) and g == 0:
                        pool.wait_ge(sig.sem, value)
                    fn(g, k)
                return step

            run(pool, POOL, {
                ("a", "mix"): a_mix, ("a", "normalise"): a_normalise, ("a", "out"): power(n0),
                ("b", "x"): once(bx, db_set, 1), ("b", "yj"): power(n1), ("b", "f"): bf, ("b", "out"): power(n2),
                ("c", "x"): cx, ("c", "f"): cf, ("c", "normalise"): c_normalise,
                ("c", "join"): once(c_join, c_loaded, LOADED["c"]), ("d", "x"): d_x,
                ("d", "ffn2"): power(n3), ("d", "norm3"): power(n4),
            })


_OUTS = [((32, 256, 256), "float32")]


def kernel(**inputs):
    import numpy as np
    import concourse.bacc as bacc
    from concourse.bass_utils import run_bass_kernel_spmd as run_spmd

    nc = bacc.Bacc("TRN2", target_bir_lowering=False, num_devices=1)
    W1 = np.asarray(inputs["L1_gnn_W"])
    D = W1.shape[0]
    columns = lambda a: np.ascontiguousarray(np.asarray(a).reshape(-1, P).T)
    T = lambda a: np.ascontiguousarray(np.asarray(a).T)
    laid = [
        ("x", inputs["x"]), ("adj", inputs["adj"]),
        ("WqT", T(inputs["L0_gnn_Wq"])), ("bq", columns(inputs["L0_gnn_bq"])),
        ("WkT", T(inputs["L0_gnn_Wk"])), ("bk", columns(inputs["L0_gnn_bk"])),
        ("WvT", T(inputs["L0_gnn_Wv"])), ("bv", columns(inputs["L0_gnn_bv"])),
        ("WoT", T(inputs["L0_gnn_Wo"])), ("bo", inputs["L0_gnn_bo"]),
        ("W1iT", T(W1[:, :D])), ("W1jT", T(W1[:, D:])), ("b1", inputs["L1_gnn_b"]),
        ("W2", inputs["L2_gnn_W"]), ("a2_src", inputs["L2_gnn_a_src"]), ("a2_dst", inputs["L2_gnn_a_dst"]),
        ("W3", inputs["L3_gnn_W_heads"]), ("a3", inputs["L3_gnn_a_heads"]),
        ("Wout", inputs["L3_gnn_W_out"]), ("aout", inputs["L3_gnn_a_out"]),
        ("Wf1", inputs["L3_gnn_w1"]), ("bf1", columns(inputs["L3_gnn_b1"])),
        ("Wf2", inputs["L3_gnn_w2"]), ("bf2", inputs["L3_gnn_b2"]),
        ("gamma", inputs["L3_gnn_ln_gamma"]), ("beta", inputs["L3_gnn_ln_beta"]),
    ]
    arrays, args = {}, []
    for name, a in laid:
        a = np.ascontiguousarray(a)
        arrays[f"in_{name}_dram"] = a
        args.append(nc.dram_tensor(f"in_{name}_dram", a.shape, mybir.dt.from_np(a.dtype), kind="ExternalInput").ap())
    for i, (shape, dtype) in enumerate(_OUTS):
        args.append(nc.dram_tensor(f"out_{i}_dram", shape, mybir.dt.from_np(np.dtype(dtype)), kind="ExternalOutput").ap())
    build(nc, *args)
    r = run_spmd(nc, [arrays], core_ids=[0])
    return r.results[0]["out_0_dram"]
```
